# Optimizing a Trainium2 kernel written in Bass

```python
import numpy as np
import jax
import jax.numpy as jnp

def _softmax(x, axis=-1):
    return jax.nn.softmax(x, axis=axis)

def _gelu(x):
    return jax.nn.gelu(x, approximate=True)

def _silu(x):
    return jax.nn.silu(x)

def _sigmoid(x):
    return jax.nn.sigmoid(x)

def _layernorm(x, axis=-1, eps=1e-05):
    m = jnp.mean(x, axis=axis, keepdims=True)
    v = jnp.var(x, axis=axis, keepdims=True)
    return (x - m) / jnp.sqrt(v + eps)

def _scatter_add(tgt, idx, src, axis=0):
    return tgt.at[idx].add(src)

def _segment_sum(src, seg, n):
    return jax.ops.segment_sum(src, seg, n)
kernel_name = 'mk_hybrid_d1_jaxref_r8_4f3e2b'

def setup_inputs(seed: int=0):
    np.random.seed(seed)
    _w = jnp.asarray

    def _L0_attn_a_setup():
        import jax, jax.numpy as jnp
        import numpy as np
        import math
        N_EMBD = 128
        N_HEAD = 16
        HEAD_SIZE = N_EMBD // N_HEAD
        LAYER_IDX = 2
        LAMBDA_INIT = 0.8 - 0.6 * math.exp(-0.3 * (LAYER_IDX - 1))
        LN_EPS = 1e-05
        B, T = (4, 128)
        key = jax.random.key(seed)
        ks = jax.random.split(key, 11)
        s = 0.02
        return {'x': jax.random.normal(ks[0], (B, T, N_EMBD), dtype=jnp.float32), 'Wq1': jax.random.normal(ks[1], (N_EMBD, N_EMBD), dtype=jnp.float32) * s, 'Wq2': jax.random.normal(ks[2], (N_EMBD, N_EMBD), dtype=jnp.float32) * s, 'Wk1': jax.random.normal(ks[3], (N_EMBD, N_EMBD), dtype=jnp.float32) * s, 'Wk2': jax.random.normal(ks[4], (N_EMBD, N_EMBD), dtype=jnp.float32) * s, 'Wv': jax.random.normal(ks[5], (N_EMBD, 2 * N_EMBD), dtype=jnp.float32) * s, 'Wc': jax.random.normal(ks[6], (2 * N_EMBD, N_EMBD), dtype=jnp.float32) * s, 'lq1': jax.random.normal(ks[7], (N_HEAD, HEAD_SIZE), dtype=jnp.float32) * 0.1, 'lk1': jax.random.normal(ks[8], (N_HEAD, HEAD_SIZE), dtype=jnp.float32) * 0.1, 'lq2': jax.random.normal(ks[9], (N_HEAD, HEAD_SIZE), dtype=jnp.float32) * 0.1, 'lk2': jax.random.normal(ks[10], (N_HEAD, HEAD_SIZE), dtype=jnp.float32) * 0.1}
    _L0_attn_a_in = _L0_attn_a_setup()

    def _L0_attn_b_setup():
        import jax, jax.numpy as jnp
        import numpy as np
        B, N, D = (2, 1024, 128)
        H, Dh = (16, 64)
        P = H * Dh
        EPS = 1e-06
        DECAY_BIAS_SHIFT = 2.0

        def _elu_plus_one(x):
            return jax.nn.elu(x) + 1.0

        def _ssd_scan(q, k, v, a, eps):
            qT = jnp.moveaxis(q, 2, 0)
            kT = jnp.moveaxis(k, 2, 0)
            vT = jnp.moveaxis(v, 2, 0)
            aT = jnp.moveaxis(a, 2, 0)
            Bb, Hh, _, Dk = q.shape
            Dv = v.shape[-1]
            S0 = jnp.zeros((Bb, Hh, Dk, Dv), q.dtype)
            z0 = jnp.zeros((Bb, Hh, Dk), q.dtype)

            def step(carry, inp):
                S, z = carry
                qt, kt, vt, at = inp
                S = at[..., None, None] * S + kt[..., :, None] * vt[..., None, :]
                z = at[..., None] * z + kt
                num = jnp.einsum('bhk,bhkv->bhv', qt, S)
                den = jnp.einsum('bhk,bhk->bh', qt, z) + eps
                return ((S, z), num / den[..., None])
            _, outT = jax.lax.scan(step, (S0, z0), (qT, kT, vT, aT))
            return jnp.moveaxis(outT, 0, 2)
        key = jax.random.key(seed)
        ks = jax.random.split(key, 7)
        s_in = 1.0 / np.sqrt(D)
        s_out = 1.0 / np.sqrt(P)
        return {'x': jax.random.normal(ks[0], (B, N, D), jnp.float32), 'Wq': jax.random.normal(ks[1], (D, P), jnp.float32) * s_in, 'Wk': jax.random.normal(ks[2], (D, P), jnp.float32) * s_in, 'Wv': jax.random.normal(ks[3], (D, P), jnp.float32) * s_in, 'Wo': jax.random.normal(ks[4], (P, D), jnp.float32) * s_out, 'Wa': jax.random.normal(ks[5], (D, H), jnp.float32) * s_in, 'ba': jnp.zeros((H,), jnp.float32)}
    _L0_attn_b_in = _L0_attn_b_setup()

    def _L0_ffn_setup():
        import jax, jax.numpy as jnp
        import numpy as np
        D_MODEL = 128
        D_FF = 512
        N_EXPERTS = 8
        TOP_K = 2
        B, T = (4, 256)
        key = jax.random.key(seed)
        ks = jax.random.split(key, 5)
        x = jax.random.normal(ks[0], (B, T, D_MODEL), dtype=jnp.float32)

        def lin(k, shape, fan_in):
            return jax.random.normal(k, shape, dtype=jnp.float32) / np.float32(np.sqrt(fan_in))
        return {'x': x, 'router_w': lin(ks[1], (N_EXPERTS, D_MODEL), D_MODEL), 'w_gate': lin(ks[2], (N_EXPERTS, D_MODEL, D_FF), D_MODEL), 'w_up': lin(ks[3], (N_EXPERTS, D_MODEL, D_FF), D_MODEL), 'w_down': lin(ks[4], (N_EXPERTS, D_FF, D_MODEL), D_FF)}
    _L0_ffn_in = _L0_ffn_setup()
    _d = {'L0_attn_a_x': _L0_attn_a_in['x'], 'L0_attn_a_Wq1': _L0_attn_a_in['Wq1'], 'L0_attn_a_Wq2': _L0_attn_a_in['Wq2'], 'L0_attn_a_Wk1': _L0_attn_a_in['Wk1'], 'L0_attn_a_Wk2': _L0_attn_a_in['Wk2'], 'L0_attn_a_Wv': _L0_attn_a_in['Wv'], 'L0_attn_a_Wc': _L0_attn_a_in['Wc'], 'L0_attn_a_lq1': _L0_attn_a_in['lq1'], 'L0_attn_a_lk1': _L0_attn_a_in['lk1'], 'L0_attn_a_lq2': _L0_attn_a_in['lq2'], 'L0_attn_a_lk2': _L0_attn_a_in['lk2'], 'L0_attn_b_Wq': _L0_attn_b_in['Wq'], 'L0_attn_b_Wk': _L0_attn_b_in['Wk'], 'L0_attn_b_Wv': _L0_attn_b_in['Wv'], 'L0_attn_b_Wo': _L0_attn_b_in['Wo'], 'L0_attn_b_Wa': _L0_attn_b_in['Wa'], 'L0_attn_b_ba': _L0_attn_b_in['ba'], 'L0_ffn_router_w': _L0_ffn_in['router_w'], 'L0_ffn_w_gate': _L0_ffn_in['w_gate'], 'L0_ffn_w_up': _L0_ffn_in['w_up'], 'L0_ffn_w_down': _L0_ffn_in['w_down']}
    _x0 = _d['L0_attn_a_x']
    _d['L0_attn_a_x'] = jax.random.normal(jax.random.fold_in(jax.random.key(seed), 1), (2, 1024, 128), dtype=_x0.dtype)
    del _x0
    return _d

def reference(L0_attn_a_x, L0_attn_a_Wq1, L0_attn_a_Wq2, L0_attn_a_Wk1, L0_attn_a_Wk2, L0_attn_a_Wv, L0_attn_a_Wc, L0_attn_a_lq1, L0_attn_a_lk1, L0_attn_a_lq2, L0_attn_a_lk2, L0_attn_b_Wq, L0_attn_b_Wk, L0_attn_b_Wv, L0_attn_b_Wo, L0_attn_b_Wa, L0_attn_b_ba, L0_ffn_router_w, L0_ffn_w_gate, L0_ffn_w_up, L0_ffn_w_down):

    def _L0_attn_a_ref(x, Wq1, Wq2, Wk1, Wk2, Wv, Wc, lq1, lk1, lq2, lk2):
        import jax, jax.numpy as jnp
        import numpy as np
        import math
        N_EMBD = 128
        N_HEAD = 16
        HEAD_SIZE = N_EMBD // N_HEAD
        LAYER_IDX = 2
        LAMBDA_INIT = 0.8 - 0.6 * math.exp(-0.3 * (LAYER_IDX - 1))
        LN_EPS = 1e-05
        B, T = (4, 128)
        Bx, Tx, C = x.shape
        H, hs = (N_HEAD, HEAD_SIZE)
        scale = 1.0 / math.sqrt(hs)
        q1 = (x @ Wq1).reshape(Bx, Tx, H, hs)
        q2 = (x @ Wq2).reshape(Bx, Tx, H, hs)
        k1 = (x @ Wk1).reshape(Bx, Tx, H, hs)
        k2 = (x @ Wk2).reshape(Bx, Tx, H, hs)
        v = (x @ Wv).reshape(Bx, Tx, H, 2 * hs)
        att1 = jnp.einsum('bqhd,bkhd->bhqk', q1, k1) * scale
        att2 = jnp.einsum('bqhd,bkhd->bhqk', q2, k2) * scale
        causal = jnp.tril(jnp.ones((Tx, Tx), dtype=bool))
        neg_inf = jnp.float32(-jnp.inf)
        att1 = jnp.where(causal, att1, neg_inf)
        att2 = jnp.where(causal, att2, neg_inf)
        a1 = jax.nn.softmax(att1, axis=-1)
        a2 = jax.nn.softmax(att2, axis=-1)
        lam1 = jnp.exp(jnp.sum(lq1 * lk1, axis=-1))
        lam2 = jnp.exp(jnp.sum(lq2 * lk2, axis=-1))
        lam_full = lam1 - lam2 + LAMBDA_INIT
        att = a1 - lam_full[None, :, None, None] * a2
        y = jnp.einsum('bhqk,bkhd->bqhd', att, v)
        mu = jnp.mean(y, axis=-1, keepdims=True)
        var = jnp.mean(jnp.square(y - mu), axis=-1, keepdims=True)
        y = (y - mu) / jnp.sqrt(var + LN_EPS)
        y = y * (1.0 - LAMBDA_INIT)
        y = y.reshape(Bx, Tx, 2 * C)
        return y @ Wc

    def _L0_attn_b_ref(x, Wq, Wk, Wv, Wo, Wa, ba):
        import jax, jax.numpy as jnp
        import numpy as np
        B, N, D = (2, 1024, 128)
        H, Dh = (16, 64)
        P = H * Dh
        EPS = 1e-06
        DECAY_BIAS_SHIFT = 2.0

        def _elu_plus_one(x):
            return jax.nn.elu(x) + 1.0

        def _ssd_scan(q, k, v, a, eps):
            qT = jnp.moveaxis(q, 2, 0)
            kT = jnp.moveaxis(k, 2, 0)
            vT = jnp.moveaxis(v, 2, 0)
            aT = jnp.moveaxis(a, 2, 0)
            Bb, Hh, _, Dk = q.shape
            Dv = v.shape[-1]
            S0 = jnp.zeros((Bb, Hh, Dk, Dv), q.dtype)
            z0 = jnp.zeros((Bb, Hh, Dk), q.dtype)

            def step(carry, inp):
                S, z = carry
                qt, kt, vt, at = inp
                S = at[..., None, None] * S + kt[..., :, None] * vt[..., None, :]
                z = at[..., None] * z + kt
                num = jnp.einsum('bhk,bhkv->bhv', qt, S)
                den = jnp.einsum('bhk,bhk->bh', qt, z) + eps
                return ((S, z), num / den[..., None])
            _, outT = jax.lax.scan(step, (S0, z0), (qT, kT, vT, aT))
            return jnp.moveaxis(outT, 0, 2)
        b, n, _ = x.shape
        q = (x @ Wq).reshape(b, n, H, Dh).transpose(0, 2, 1, 3)
        k = (x @ Wk).reshape(b, n, H, Dh).transpose(0, 2, 1, 3)
        v = (x @ Wv).reshape(b, n, H, Dh).transpose(0, 2, 1, 3)
        q = _elu_plus_one(q)
        k = _elu_plus_one(k)
        a = jax.nn.sigmoid(x @ Wa + ba + DECAY_BIAS_SHIFT)
        a = a.transpose(0, 2, 1)
        out = _ssd_scan(q, k, v, a, EPS)
        out = out.transpose(0, 2, 1, 3).reshape(b, n, P)
        return out @ Wo

    def _L0_ffn_ref(x, router_w, w_gate, w_up, w_down):
        import jax, jax.numpy as jnp
        import numpy as np
        D_MODEL = 128
        D_FF = 512
        N_EXPERTS = 8
        TOP_K = 2
        B, T = (4, 256)
        Bx, Tx, D = x.shape
        xf = x.reshape(-1, D)
        logits = xf @ router_w.T
        scores = jax.nn.softmax(logits, axis=-1)
        topk_scores, topk_ids = jax.lax.top_k(scores, TOP_K)
        topk_scores = topk_scores / topk_scores.sum(-1, keepdims=True)
        cw = (jax.nn.one_hot(topk_ids, N_EXPERTS, dtype=xf.dtype) * topk_scores[..., None]).sum(1)

        def body(acc, inputs):
            wg, wu, wd, w = inputs
            h = jax.nn.silu(xf @ wg) * (xf @ wu)
            acc = acc + w[:, None] * (h @ wd)
            return (acc, None)
        out, _ = jax.lax.scan(body, jnp.zeros_like(xf), (w_gate, w_up, w_down, cw.T))
        return out.reshape(Bx, Tx, D)
    x = L0_attn_a_x
    x = x + _L0_attn_a_ref(_layernorm(x, axis=-1), L0_attn_a_Wq1, L0_attn_a_Wq2, L0_attn_a_Wk1, L0_attn_a_Wk2, L0_attn_a_Wv, L0_attn_a_Wc, L0_attn_a_lq1, L0_attn_a_lk1, L0_attn_a_lq2, L0_attn_a_lk2)
    x = x + _L0_ffn_ref(_layernorm(x, axis=-1), L0_ffn_router_w, L0_ffn_w_gate, L0_ffn_w_up, L0_ffn_w_down)
    x = x + _L0_attn_b_ref(_layernorm(x, axis=-1), L0_attn_b_Wq, L0_attn_b_Wk, L0_attn_b_Wv, L0_attn_b_Wo, L0_attn_b_Wa, L0_attn_b_ba)
    x = x + _L0_ffn_ref(_layernorm(x, axis=-1), L0_ffn_router_w, L0_ffn_w_gate, L0_ffn_w_up, L0_ffn_w_down)
    return x

_drawn_inputs = setup_inputs


def setup_inputs(seed=0):
    import zlib

    import numpy as np

    out = dict(_drawn_inputs(seed))
    spreads = {'L0_attn_b_ba': (0.0, 0.283)}
    factors = {'L0_attn_a_lq1': 3.468, 'L0_attn_a_lk1': 3.611}
    for name, (base, spread) in spreads.items():
        noise = np.random.default_rng([zlib.crc32(name.encode()), seed]).standard_normal(out[name].shape)
        drawn = base * np.exp(spread * noise) if base else spread * noise
        out[name] = jnp.asarray(drawn.astype(out[name].dtype))
    for name, factor in factors.items():
        out[name] = (out[name] * factor).astype(out[name].dtype)
    return out
```

```python
import math
from contextlib import ExitStack

import concourse.bass as bass
from concourse import mybir

F32 = mybir.dt.float32
BF16 = mybir.dt.bfloat16
U32 = mybir.dt.uint32
ALU = mybir.AluOpType
ACT = mybir.ActivationFunctionType
AX = mybir.AxisListType

P = 128
LAMBDA_INIT = 0.8 - 0.6 * math.exp(-0.3 * (2 - 1))
LN_EPS = 1e-5
NEG = -1e30


class Chain:

    def __init__(self, eng, sem, base=0):
        self.eng, self.sem, self.n, self.base = eng, sem, 0, base

    def link(self, ins):
        self.n += 1
        ins.then_inc(self.sem, 1)
        self.eng.wait_ge(self.sem, self.base + self.n)


def from_(t, lo):
    return not isinstance(t, int) or t >= lo


def over_pairs(eng, lo, hi, body):
    pairs = (hi - lo) // 2
    with eng.Fori(0, pairs) as it:
        for k in range(2):
            body(it * 2 + (lo + k), (lo + k) % 2)
    for s in range(lo + 2 * pairs, hi):
        body(s, s % 2)


def layer_norm(nc, tag, X, XN, XNT, ident, NT, x_loaded=None):
    with ExitStack() as ctx:
        stats = ctx.enter_context(nc.sbuf_tensor(f"{tag}_stats", [P, NT, 6], F32))
        mv = ctx.enter_context(nc.sbuf_tensor(f"{tag}_mv", [P, NT, 2], F32))
        ve = ctx.enter_context(nc.sbuf_tensor(f"{tag}_ve", [P, NT], F32))
        sd = ctx.enter_context(nc.sbuf_tensor(f"{tag}_sd", [P, NT], F32))
        rstd = ctx.enter_context(nc.sbuf_tensor(f"{tag}_rstd", [P, NT], F32))
        tp = ctx.enter_context(nc.psum_tensor(f"{tag}_tp", [P, 2, 512], F32))
        dve_step = nc.alloc_semaphore(f"{tag}_dve_step")
        var_ready = nc.alloc_semaphore(f"{tag}_var_ready")
        sd_ready = nc.alloc_semaphore(f"{tag}_sd_ready")
        xn_ready = nc.alloc_semaphore(f"{tag}_xn_ready")
        tp_ready = nc.alloc_semaphore(f"{tag}_tp_ready")
        tp_free = nc.alloc_semaphore(f"{tag}_tp_free")
        block = ctx.enter_context(nc.Block())

        @block.vector
        def _(dve):
            chain = Chain(dve, dve_step)
            for t in range(NT):
                if x_loaded is not None and t % 4 == 0:
                    dve.wait_ge(x_loaded[t // 4], 16)
                last = nc.vector.bn_stats(stats[:, t, :], X[:, t, :])
            chain.link(last)
            for t in range(NT):
                last = nc.vector.bn_aggr(mv[:, t, :], stats[:, t, :])
            chain.link(last)
            nc.vector.tensor_scalar_add(ve[:], mv[:, :, 1], LN_EPS).then_inc(var_ready, 1)
            dve.wait_ge(sd_ready, 1)
            chain.link(nc.vector.reciprocal(rstd[:], sd[:]))
            for t in range(NT):
                nc.vector.tensor_scalar(XN[:, t, :], X[:, t, :], mv[:, t, 0:1], rstd[:, t:t + 1],
                                        ALU.subtract, ALU.mult).then_inc(xn_ready, 1)

        @block.scalar
        def _(act):
            act.wait_ge(var_ready, 1)
            nc.scalar.activation(sd[:], ve[:], ACT.Sqrt).then_inc(sd_ready, 1)
            for q in range(NT // 4):
                act.wait_ge(tp_ready, q + 1)
                nc.scalar.activation(XNT[:, q * 512:(q + 1) * 512], tp[:, q % 2, :], ACT.Copy).then_inc(tp_free, 1)

        @block.tensor
        def _(pe):
            for t in range(NT):
                q = t // 4
                if t % 4 == 0 and q >= 2:
                    pe.wait_ge(tp_free, q - 1)
                pe.wait_ge(xn_ready, t + 1)
                last = nc.tensor.transpose(tp[:, q % 2, (t % 4) * P:(t % 4 + 1) * P], XN[:, t, :], ident[:])
                if t % 4 == 3:
                    last.then_inc(tp_ready, 1)


def diff_attention(nc, X, W3, ident, identb, io, scratch, load_next):
    NB, NTOK, D, H, HS = 2, 1024, 128, 16, 8
    NT = NB * NTOK // P
    KB = NTOK // P
    G = NB * H // 2
    U = 4
    VW = 32
    PARTS = ((0, 0), (0, 1), (1, 0), (1, 1), (0, 2), (2, 0))
    KR = 8 * len(PARTS)
    MR = P - 2
    KQ = P
    SC = 1.0 / math.sqrt(HS)
    QK = scratch["qk"]

    with ExitStack() as ctx:
        def sb(name, shape, dt=F32):
            return ctx.enter_context(nc.sbuf_tensor(name, shape, dt))

        def sem(name):
            return nc.alloc_semaphore(name)

        VP = sb("VP", [P, G, KB, 2, VW])
        OT = sb("OT", [P, G, NTOK])
        lam = sb("lam", [P, H])

        with ExitStack() as c2:
            XNT = c2.enter_context(nc.sbuf_tensor("a_XNT", [P, NT * P], F32))
            W = c2.enter_context(nc.sbuf_tensor("a_W", [P, 4, P], F32))
            WV = c2.enter_context(nc.sbuf_tensor("a_WV", [P, 2 * P], F32))
            LQ = c2.enter_context(nc.sbuf_tensor("a_LQ", [P, 4, H, HS], F32))
            lp = c2.enter_context(nc.sbuf_tensor("a_lp", [P, 2, H, HS], F32))
            ls = c2.enter_context(nc.sbuf_tensor("a_ls", [P, 2, H], F32))
            le = c2.enter_context(nc.sbuf_tensor("a_le", [P, 2, H], F32))
            w_loaded = nc.alloc_semaphore("a_w_loaded")
            x_loaded = [nc.alloc_semaphore(f"a_x_loaded{i}") for i in range(4)]
            parts = c2.enter_context(nc.sbuf_tensor("a_parts", [P, 3, 3, 512], BF16))
            rest = c2.enter_context(nc.sbuf_tensor("a_rest", [P, 3, 512], F32))
            with ExitStack() as c3:
                XN = c3.enter_context(nc.sbuf_tensor("a_XN", [P, NT, D], F32))
                with nc.Block() as blk:
                    @blk.sync
                    def _(sp):
                        xv = io["x"].rearrange("b (t p) d -> p (b t) d", p=P)
                        for c in range(4):
                            sp.dma_start(X[:, 4 * c:4 * c + 4, :], xv[:, 4 * c:4 * c + 4, :]).then_inc(x_loaded[c], 16)
                        for i, n in enumerate(("Wq1", "Wk1", "Wq2", "Wk2")):
                            sp.dma_start(W[:, i, :], io[n]).then_inc(w_loaded, 16)
                        sp.dma_start(WV[:], io["Wv"]).then_inc(w_loaded, 16)
                        for i, n in enumerate(("lq1", "lk1", "lq2", "lk2")):
                            sp.dma_start(LQ[:, i], io[n].partition_broadcast(P)).then_inc(w_loaded, 16)
                layer_norm(nc, "lna", X, XN, XNT, ident, NT, x_loaded)

            pp = c2.enter_context(nc.psum_tensor("a_pp", [P, 3, 512], F32))
            pv = c2.enter_context(nc.psum_tensor("a_pv", [P, 2, 512], F32))

            def s2(name):
                return nc.alloc_semaphore(name)

            qk_ready, qk_free, p0_ready, rest_ready, p1_ready, p2_ready = map(
                s2, ("a_qk_ready", "a_qk_free", "a_p0_ready", "a_rest_ready", "a_p1_ready", "a_p2_ready"))
            parts_stored = [s2(f"a_parts_stored{i}") for i in range(3)]
            v_ready, v_free, vpad, chain_s, lsum_ready, lexp_ready = map(
                s2, ("a_v_ready", "a_v_free", "a_vpad", "a_chain", "a_lsum_ready", "a_lexp_ready"))
            items = [(att, qk, b, c) for b in range(NB) for att in range(2) for qk in range(2) for c in range(2)]
            with nc.Block() as block:
                @block.tensor
                def _(pe):
                    pe.wait_ge(w_loaded, 16 * 9)
                    for n, (att, qk, b, c) in enumerate(items):
                        if n >= 3:
                            pe.wait_ge(rest_ready, n - 2)
                        nc.tensor.matmul(pp[:, n % 3, :], W[:, 2 * att + qk, :],
                                         XNT[:, b * NTOK + c * 512:b * NTOK + c * 512 + 512],
                                         start=True, stop=True).then_inc(qk_ready, 1)
                    for t in range(NT):
                        if t >= 2:
                            pe.wait_ge(v_free, t - 1)
                        nc.tensor.matmul(pv[:, t % 2, 0:2 * P], XNT[:, t * P:(t + 1) * P], WV[:],
                                         start=True, stop=True).then_inc(v_ready, 1)

                @block.scalar
                def _(act):
                    act.wait_ge(lsum_ready, 1)
                    nc.scalar.activation(le[:], ls[:], ACT.Exp).then_inc(lexp_ready, 1)
                    for n in range(len(items)):
                        act.wait_ge(qk_ready, n + 1)
                        if n >= 3:
                            act.wait_ge(parts_stored[n % 3], 16 * 8 * (n // 3))
                        nc.scalar.activation(parts[:, n % 3, 0, :], pp[:, n % 3, :], ACT.Copy).then_inc(p0_ready, 1)
                        act.wait_ge(rest_ready, n + 1)
                        nc.scalar.activation(parts[:, n % 3, 1, :], rest[:, n % 3, :], ACT.Copy).then_inc(p1_ready, 1)
                    act.wait_ge(vpad, 2)
                    for t in range(NT):
                        b, kb = divmod(t, KB)
                        act.wait_ge(v_ready, t + 1)
                        nc.scalar.activation(VP[:, b * 8:(b + 1) * 8, kb, :, 0:16],
                                             pv[:, t % 2, 0:2 * P].rearrange("p (g h v) -> p g h v", g=8, h=2),
                                             ACT.Copy).then_inc(v_free, 1)

                @block.vector
                def _(dve):
                    chain = Chain(dve, chain_s)
                    dve.wait_ge(w_loaded, 16 * 9)
                    nc.vector.tensor_tensor(lp[:, 0], LQ[:, 0], LQ[:, 1], ALU.mult)
                    chain.link(nc.vector.tensor_tensor(lp[:, 1], LQ[:, 2], LQ[:, 3], ALU.mult))
                    nc.vector.reduce_sum(ls[:], lp[:], AX.X).then_inc(lsum_ready, 1)
                    dve.wait_ge(lexp_ready, 1)
                    chain.link(nc.vector.tensor_tensor(lam[:], le[:, 0], le[:, 1], ALU.subtract))
                    chain.link(nc.vector.tensor_scalar_add(lam[:], lam[:], LAMBDA_INIT))
                    for n in range(len(items)):
                        dve.wait_ge(p0_ready, n + 1)
                        if n >= 3:
                            dve.wait_ge(p2_ready, n - 2)
                        nc.vector.tensor_tensor(rest[:, n % 3, :], pp[:, n % 3, :], parts[:, n % 3, 0, :],
                                                ALU.subtract).then_inc(rest_ready, 1)

                @block.gpsimd
                def _(pool):
                    nc.gpsimd.memset(VP[:], 0.0).then_inc(vpad, 1)
                    pool.wait_ge(vpad, 1)
                    nc.gpsimd.memset(VP[:, :, :, :, 16:17], 1.0).then_inc(vpad, 1)
                    for n in range(len(items)):
                        pool.wait_ge(p1_ready, n + 1)
                        nc.gpsimd.tensor_tensor(parts[:, n % 3, 2, :], rest[:, n % 3, :], parts[:, n % 3, 1, :],
                                                ALU.subtract).then_inc(p2_ready, 1)

                @block.sync
                def _(sp):
                    for n, (att, qk, b, c) in enumerate(items):
                        sp.wait_ge(p2_ready, n + 1)
                        for hp in range(8):
                            dst = QK[qk, :, b * 8 + hp, att, :, :, c * 512:(c + 1) * 512]
                            sp.dma_start(dst.rearrange("p h d n -> (h d) p n"),
                                         parts[16 * hp:16 * hp + 16, n % 3]).then_inc(parts_stored[n % 3], 16)
                    for i in range(3):
                        sp.wait_ge(parts_stored[i], 16 * 8 * len(items[i::3]))

        with ExitStack() as c2:
            def s2(name):
                return nc.alloc_semaphore(name)

            NQ = 3
            half = NQ * U * NTOK // 2
            QS, KS = (W3[:, i * half:(i + 1) * half].bitcast(BF16).rearrange("p (s u n) -> p s u n", s=NQ, u=U)
                      for i in range(2))
            VS = c2.enter_context(nc.sbuf_tensor("VS", [P, NQ, KB, 2, VW], F32))
            NPB = 8
            PB = c2.enter_context(nc.sbuf_tensor("PB", [P, NPB, 512], F32))
            maskb = c2.enter_context(nc.sbuf_tensor("maskb", [P, P], BF16))
            mx = c2.enter_context(nc.sbuf_tensor("mx", [P, 2, U, KB], F32))
            mxc = c2.enter_context(nc.sbuf_tensor("mxc", [P, U * KB], F32))
            mrow = c2.enter_context(nc.sbuf_tensor("mrow", [U * KB, 2, P], BF16))
            S1 = c2.enter_context(nc.psum_tensor("S1", [P, 3, 512], F32))
            S2 = c2.enter_context(nc.psum_tensor("S2", [P, 3, 512], F32))
            PV = c2.enter_context(nc.psum_tensor("PV", [P, 2, 512], F32))
            pool_init = s2("b_pool_init")
            const_s, g_loaded = s2("b_const"), [s2(f"g_loaded{i}") for i in range(NQ)]
            s1_done, s1_free, m_rows, mdve = map(
                s2, ("s1_done", "s1_free", "m_rows", "mdve"))
            s2_done, exp_done, mask_done, pv_done, pv_free, m_part = map(
                s2, ("s2_done", "exp_done", "mask_done", "pv_done", "pv_free", "m_part"))
            t1 = [(qb, c, u, min(512, (qb + 1) * P - c * 512)) for qb in range(KB)
                  for c in range(2) if (qb + 1) * P > c * 512 for u in range(U)]
            t2 = [(kb, c, u, max(kb * P, c * 512)) for kb in range(KB) for c in range(2) if kb * P < (c + 1) * 512
                  for u in range(U)]
            N1, N2 = len(t1) + 1, len(t2)
            ND = sum(1 for kb, c, u, q0 in t2 if q0 == kb * P and kb // 4 == c)
            NLOAD = 16 * (2 * len(PARTS) + 1)
            diag_at = {}
            for i, (kb, c, u, q0) in enumerate(t2):
                if kb // 4 == c:
                    diag_at[i] = len(diag_at)
            assert len(t1) == N2 and N2 % NPB == 0 and N2 % 3 == 0 and len(diag_at) == ND and G % 3 == 1
            gate = c2.enter_context(nc.sbuf_tensor("gate", [P, ND], F32))

            with nc.Block() as block:
                @block.sync
                def _(sp):
                    sp.wait_ge(const_s, 5)

                    def load(g, s):
                        for r, (pq, pk) in enumerate(PARTS):
                            for qk, dst, part in ((0, QS, pq), (1, KS, pk)):
                                src = QK[qk, part, bass.ds(g, 1)].rearrange("o a h d n -> d (o a h) n")
                                sp.dma_start(dst[8 * r:8 * r + 8, s], src).then_inc(g_loaded[s], 16)
                        sp.dma_start(VS[:, s], VP[:, bass.ds(g, 1)].rearrange("p o k h v -> p (o k) h v"))\
                          .then_inc(g_loaded[s], 16)

                    def m_store(g, s):
                        sp.wait_ge(s1_free, (g + 1) * N1)
                        for t in range(2):
                            sp.dma_start(QS[MR + t:MR + t + 1, s].rearrange("t u (k q) -> t (u k) q", q=P),
                                         mrow[:, t]).then_inc(m_rows, 16)

                    load(0, 0)
                    load(1, 1)
                    m_store(0, 0)
                    with sp.Fori(0, (G - 4) // 3) as it:
                        for k in range(3):
                            g = it * 3 + k
                            sp.wait_ge(pv_free, g + 1)
                            load(g + 2, (k + 2) % 3)
                            m_store(g + 1, (k + 1) % 3)
                    for g in range(G - 4, G - 1):
                        if g + 2 < G:
                            sp.wait_ge(pv_free, g + 1)
                            load(g + 2, (g + 2) % 3)
                        m_store(g + 1, (g + 1) % 3)

                @block.tensor
                def _(pe):
                    pe.wait_ge(const_s, 5)

                    def max_tile(g, s, i, first=False):
                        if not (first and i < 3):
                            pe.wait_ge(s1_free, g * N1 + max(i - 2, 0))
                        qb, c, u, n = t1[i]
                        diag = n + c * 512 == (qb + 1) * P
                        ins = nc.tensor.matmul(S1[:, i % 3, 0:n], QS[0:MR, s, u, qb * P:(qb + 1) * P],
                                               KS[0:MR, s, u, c * 512:c * 512 + n], start=True, stop=not diag)
                        if diag:
                            ins = nc.tensor.matmul(S1[:, i % 3, n - P:n], identb[:], maskb[:], start=False, stop=True)
                        ins.then_inc(s1_done, 1)

                    def max_turn(g):
                        pe.wait_ge(m_part, g + 1)
                        nc.tensor.transpose(S1[0:U * KB, 0, 0:P], mxc[:], ident[:]).then_inc(s1_done, 1)

                    def score_tile(g, s, i):
                        kb, c, u, q0 = t2[i]
                        if i >= 3:
                            pe.wait_ge(exp_done, g * N2 + (i - 2))
                        nc.tensor.matmul(S2[:, i % 3, 0:(c + 1) * 512 - q0], KS[:, s, u, kb * P:(kb + 1) * P],
                                         QS[:, s, u, q0:(c + 1) * 512], start=True, stop=True).then_inc(s2_done, 1)

                    def value_tile(g, s, i):
                        kb, c, u, q0 = t2[i]
                        if i == 0:
                            pe.wait_ge(pv_free, g + 1)
                        pe.wait_ge(exp_done, g * N2 + (i + 1))
                        if i in diag_at:
                            pe.wait_ge(mask_done, g * ND + (diag_at[i] + 1))
                        nc.tensor.matmul(PV[32 * u:32 * u + 32, c, q0 - c * 512:512], VS[:, s, kb, u % 2, :],
                                         PB[:, i % NPB, 0:(c + 1) * 512 - q0], start=(kb == 0),
                                         stop=(kb == 4 * c + 3)).then_inc(pv_done, 1)

                    def step(g, s, next_loads):
                        pe.wait_ge(m_rows, (g + 1) * 32)
                        if next_loads is not None:
                            pe.wait_ge(g_loaded[(s + 1) % 3], next_loads * NLOAD)
                        for i in range(N2):
                            if next_loads is not None:
                                max_tile(g + 1, (s + 1) % 3, i)
                            score_tile(g, s, i)
                            if i % U == 1 and i > U:
                                for j in range(i - U - 1, i - 1):
                                    value_tile(g, s, j)
                        if next_loads is not None:
                            max_turn(g + 1)
                        for j in range(N2 - U, N2):
                            value_tile(g, s, j)

                    pe.wait_ge(g_loaded[0], NLOAD)
                    for i in range(N2):
                        max_tile(0, 0, i, first=True)
                    max_turn(0)
                    with pe.Fori(0, (G - 1) // 3) as it:
                        for k in range(3):
                            step(it * 3 + k, k, it + 1 if k < 2 else it + 2)
                    step(G - 1, (G - 1) % 3, None)

                @block.scalar
                def _(act):
                    with act.Fori(0, G) as g:
                        for i, (kb, c, u, q0) in enumerate(t2):
                            n = (c + 1) * 512 - q0
                            act.wait_ge(s2_done, g * N2 + (i + 1))
                            if i >= NPB:
                                act.wait_ge(pv_done, g * N2 + (i - NPB + 1))
                            nc.scalar.activation(PB[:, i % NPB, 0:n], S2[:, i % 3, 0:n], ACT.Exp, scale=SC)\
                              .then_inc(exp_done, 1)
                        act.wait_ge(pv_done, (g + 1) * N2)
                        nc.scalar.activation(OT[:, bass.ds(g, 1), :].rearrange("p o (c n) -> p (o c) n", c=2), PV[:], ACT.Copy)\
                          .then_inc(pv_free, 1)

                @block.gpsimd
                def _(pool):
                    nc.gpsimd.memset(maskb[:], 0.0).then_inc(pool_init, 1)
                    pool.wait_ge(pool_init, 1)
                    nc.gpsimd.affine_select(out=maskb[:], in_=maskb[:], compare_op=ALU.is_ge, fill=NEG, base=0,
                                            pattern=[[-1, P]], channel_multiplier=1).then_inc(const_s, 1)
                    with pool.Fori(0, G) as g:
                        for i in sorted(diag_at):
                            pool.wait_ge(exp_done, g * N2 + (i + 1))
                            nc.gpsimd.tensor_tensor(gate[:, diag_at[i]:diag_at[i] + 1], ident[:, 0:1], ident[:, 0:1], ALU.add)
                            nc.gpsimd.affine_select(out=PB[:, i % NPB, 0:P], in_=PB[:, i % NPB, 0:P],
                                                    compare_op=ALU.is_ge, fill=0.0, base=0, pattern=[[1, P]],
                                                    channel_multiplier=-1).then_inc(mask_done, 1)

                @block.vector
                def _(dve):
                    nc.vector.memset(mx[:], NEG).then_inc(const_s, 1)
                    nc.vector.memset(PV[:, 0, 0:1], 0.0).then_inc(pv_free, 1)
                    nc.vector.memset(W3[:, 0:half].bitcast(U32), 0).then_inc(const_s, 1)
                    nc.vector.memset(W3[0:96, half:2 * half].bitcast(U32), 0).then_inc(const_s, 1)
                    nc.vector.memset(KS[96:P].rearrange("p s u n -> p (s u n)"), 1.0).then_inc(const_s, 1)
                    dve.wait_ge(const_s, 5)
                    with dve.Fori(0, G) as g:
                        for i, (qb, c, u, n) in enumerate(t1):
                            dve.wait_ge(s1_done, g * N1 + (i + 1))
                            last = nc.vector.reduce_max(mx[:, c, u, qb:qb + 1], S1[:, i % 3, 0:n], AX.X)
                            last.then_inc(s1_free, 1)
                        dve.wait_ge(s1_free, g * N1 + len(t1))
                        nc.vector.tensor_tensor(mxc[:], mx[:, 0].rearrange("p u k -> p (u k)"),
                                                mx[:, 1].rearrange("p u k -> p (u k)"), ALU.max).then_inc(m_part, 1)
                        dve.wait_ge(s1_done, (g + 1) * N1)
                        nc.vector.tensor_scalar(mrow[:, 0], S1[0:U * KB, 0, 0:P], -1.0, None, ALU.mult)\
                          .then_inc(mdve, 1)
                        dve.wait_ge(mdve, g + 1)
                        nc.vector.scalar_tensor_tensor(out=mrow[:, 1], in0=S1[0:U * KB, 0, 0:P], scalar=-1.0,
                                                       in1=mrow[:, 0], op0=ALU.mult, op1=ALU.subtract)\
                          .then_inc(s1_free, 1)


        with ExitStack() as c2:
            def sb2(name, shape, dt=F32):
                return c2.enter_context(nc.sbuf_tensor(name, shape, dt))

            def s2(name):
                return nc.alloc_semaphore(name)

            NP = NT // 2
            WC = sb2("WC", [P, 2, P])
            rd = sb2("rd", [P, 16, 2, 2])
            y1, y2, yc, sq, yn = (sb2(n, [P, 16, 2, 16]) for n in ("y1", "y2", "yc", "sq", "yn"))
            mean, var, sd, rs = (sb2(n, [P, 16, 2]) for n in ("mean", "var", "sd", "rs"))
            ynT = sb2("ynT", [P, 4, P])
            TP = c2.enter_context(nc.psum_tensor("TP", [P, 16, 2, 2, 32], F32))
            YT = c2.enter_context(nc.psum_tensor("YT", [P, 4, P], F32))
            OC = c2.enter_context(nc.psum_tensor("OC", [P, 512], F32))
            wc_loaded, tp_done, tp_free, c_step, var_ready, sd_ready, yn_ready, yt_done, ynt_ready, oc_done, x_added = map(
                s2, ("wc_loaded", "tp_done", "tp_free", "c_step", "c_var", "c_sd", "yn_ready", "yt_done", "ynt_ready",
                     "oc_done", "x_added"))
            with nc.Block() as block:
                @block.sync
                def _(sp):
                    sp.dma_start(WC[:], io["Wc"].rearrange("(k p) n -> p k n", p=P)).then_inc(wc_loaded, 16)
                    load_next(sp)

                @block.tensor
                def _(pe):
                    pe.wait_ge(wc_loaded, 16)
                    for pr in range(NP + 1):
                        if pr < NP:
                            if pr:
                                pe.wait_ge(tp_free, pr)
                            for t in range(2):
                                b, qb = divmod(2 * pr + t, KB)
                                for hp in range(8):
                                    last = nc.tensor.transpose(
                                        TP[:, 8 * t + hp].rearrange("p a h v -> p (a h v)"),
                                        OT[:, b * 8 + hp, qb * P:(qb + 1) * P], ident[:])
                            last.then_inc(tp_done, 1)
                        if pr:
                            pe.wait_ge(yn_ready, pr)
                            for j in range(4):
                                last = nc.tensor.transpose(YT[:, j], yn[:].rearrange("p k h v -> p (k h v)")[:, j * P:(j + 1) * P], ident[:])
                            last.then_inc(yt_done, 1)
                            pe.wait_ge(ynt_ready, pr)
                            if pr > 1:
                                pe.wait_ge(x_added, pr - 1)
                            for t in range(2):
                                for k in range(2):
                                    last = nc.tensor.matmul(OC[:, t * P:(t + 1) * P], ynT[:, 2 * t + k], WC[:, k],
                                                            start=(k == 0), stop=(k == 1))
                            last.then_inc(oc_done, 1)

                @block.scalar
                def _(act):
                    for pr in range(NP):
                        act.wait_ge(var_ready, pr + 1)
                        nc.scalar.activation(sd[:], var[:], ACT.Sqrt).then_inc(sd_ready, 1)
                        act.wait_ge(yt_done, pr + 1)
                        nc.scalar.activation(ynT[:], YT[:], ACT.Copy).then_inc(ynt_ready, 1)

                @block.vector
                def _(dve):
                    chain = Chain(dve, c_step)

                    def over_values(ap):
                        return ap.unsqueeze(3).to_broadcast([P, 16, 2, 16])

                    lam_b = lam[:].rearrange("p (k h) -> p k h", h=2).unsqueeze(1).to_broadcast([P, 2, 8, 2])

                    def add_out(pr):
                        dve.wait_ge(oc_done, pr + 1)
                        xs = X[:, 2 * pr:2 * pr + 2, :].rearrange("p t d -> p (t d)")
                        nc.vector.tensor_tensor(xs, xs, OC[:, 0:2 * P], ALU.add).then_inc(x_added, 1)

                    for pr in range(NP):
                        dve.wait_ge(tp_done, pr + 1)
                        chain.link(nc.vector.reciprocal(rd[:], TP[:, :, :, :, 16]))
                        r2 = rd[:, :, 1, :].rearrange("p (t k) h -> p t k h", t=2)
                        chain.link(nc.vector.tensor_tensor(r2, r2, lam_b, ALU.mult))
                        nc.vector.tensor_tensor(y1[:], TP[:, :, 0, :, 0:16], over_values(rd[:, :, 0, :]), ALU.mult)
                        ins = nc.vector.tensor_tensor(y2[:], TP[:, :, 1, :, 0:16], over_values(rd[:, :, 1, :]), ALU.mult)
                        ins.then_inc(tp_free, 1)
                        dve.wait_ge(tp_free, pr + 1)
                        chain.link(nc.vector.tensor_tensor(y1[:], y1[:], y2[:], ALU.subtract))
                        chain.link(nc.vector.reduce_sum(mean[:], y1[:], AX.X))
                        chain.link(nc.vector.tensor_scalar(mean[:], mean[:], 1.0 / 16, None, ALU.mult))
                        chain.link(nc.vector.tensor_tensor(yc[:], y1[:], over_values(mean[:]), ALU.subtract))
                        chain.link(nc.vector.tensor_tensor(sq[:], yc[:], yc[:], ALU.mult))
                        chain.link(nc.vector.reduce_sum(var[:], sq[:], AX.X))
                        nc.vector.tensor_scalar(var[:], var[:], 1.0 / 16, LN_EPS, ALU.mult, ALU.add).then_inc(var_ready, 1)
                        if pr:
                            add_out(pr - 1)
                        dve.wait_ge(sd_ready, pr + 1)
                        chain.link(nc.vector.reciprocal(rs[:], sd[:]))
                        chain.link(nc.vector.tensor_scalar(rs[:], rs[:], 1.0 - LAMBDA_INIT, None, ALU.mult))
                        dve.wait_ge(yt_done, pr)
                        nc.vector.tensor_tensor(yn[:], yc[:], over_values(rs[:]), ALU.mult).then_inc(yn_ready, 1)
                    add_out(NP - 1)


class Router:
    E, TOPK, FF = 8, 2, 512
    NT = 16
    SLOTS = NT * TOPK + E - 1


def load_experts(nc, sp, W3, io, loaded):
    E, FF = Router.E, Router.FF
    n = E * FF
    for i, name in enumerate(("w_gate", "w_up")):
        sp.dma_start(W3[:, i * n:(i + 1) * n].rearrange("p (e f) -> p e f", e=E),
                     io[name].rearrange("e p f -> p e f")).then_inc(loaded, 16)
    sp.dma_start(W3[:, 2 * n:3 * n].rearrange("p (e k d) -> p e k d", e=E, d=P),
                 io["w_down"].rearrange("e (k p) d -> p e k d", p=P)).then_inc(loaded, 16)


def moe(nc, tag, X, W3, ident, io, scratch, experts_loaded):
    E, FF, NT, SLOTS = Router.E, Router.FF, Router.NT, Router.SLOTS
    FK = FF // P
    XS, YS = scratch["xs"], scratch["ys"]
    n = E * FF
    WG, WU = (W3[:, i * n:(i + 1) * n].rearrange("p (e f) -> p e f", e=E) for i in range(2))
    WD = W3[:, 2 * n:3 * n].rearrange("p (e k d) -> p e k d", e=E, d=P)

    with ExitStack() as ctx:
        def sb(name, shape, dt=F32):
            return ctx.enter_context(nc.sbuf_tensor(f"{tag}_{name}", shape, dt))

        def sem(name):
            return nc.alloc_semaphore(f"{tag}_{name}")

        wts = sb("wts", [P, 2, NT])
        posu = sb("posu", [P, 2, NT], U32)
        etab = sb("etab", [1, SLOTS], U32)
        with ExitStack() as c2:
            def sb2(name, shape, dt=F32):
                return c2.enter_context(nc.sbuf_tensor(f"{tag}_{name}", shape, dt))

            def s2(name):
                return nc.alloc_semaphore(f"{tag}_{name}")

            XN = sb2("XN", [P, NT, P])
            XNT = sb2("XNT", [P, NT * P])
            layer_norm(nc, tag + "_ln", X, XN, XNT, ident, NT)

            RW = sb2("RW", [P, E])
            tri = sb2("tri", [P, P])
            ones = sb2("ones", [P, P])
            ioe = sb2("ioe", [P, E])
            iot = sb2("iot", [P, NT])
            ios = sb2("ios", [1, SLOTS])
            z, ex, prob, M, cnt, cinc, pos = (sb2(k, [P, NT, E]) for k in ("z", "ex", "prob", "M", "cnt", "cinc", "pos"))
            lmax, lsum, lrec, wsum, wrec = (sb2(k, [P, NT]) for k in ("lmax", "lsum", "lrec", "wsum", "wrec"))
            top = sb2("top", [P, NT, 8])
            tid = sb2("tid", [P, NT, 8], U32)
            tidf = sb2("tidf", [P, 2, NT])
            OH = sb2("OH", [P, 2, NT, E])
            sel = sb2("sel", [P, 2, NT, E])
            posf = sb2("posf", [P, 2, NT])
            over = sb2("over", [P, E, NT])
            tiles, ends, base = (sb2(k, [P, E]) for k in ("tiles", "ends", "base"))
            sover = sb2("sover", [1, SLOTS, E])
            sef = sb2("sef", [1, SLOTS])
            LG = c2.enter_context(nc.psum_tensor(f"{tag}_LG", [P, 512], F32))
            RC = c2.enter_context(nc.psum_tensor(f"{tag}_RC", [P, 4, NT, E], F32))
            rw_loaded, const_r, r_step, lg_done, z_ready, ex_ready, m_ready, rc_done, pos_ready, scattered = map(
                s2, ("rw_loaded", "const_r", "r_step", "lg_done", "z_ready", "ex_ready", "m_ready", "rc_done", "pos_ready",
                     "scattered"))
            with nc.Block() as block:
                @block.sync
                def _(sp):
                    with nc.allow_non_contiguous_dma("router weights, 4 KiB"):
                        sp.dma_start(RW[:], io["router_w"].rearrange("e d -> d e")).then_inc(rw_loaded, 16)

                @block.gpsimd
                def _(pool):
                    nc.gpsimd.iota(ioe[:], [[1, E]], base=0, channel_multiplier=0,
                                   allow_small_or_imprecise_dtypes=True).then_inc(const_r, 1)
                    nc.gpsimd.iota(iot[:], [[P, NT]], base=0, channel_multiplier=0,
                                   allow_small_or_imprecise_dtypes=True).then_inc(const_r, 1)
                    nc.gpsimd.iota(ios[:], [[1, SLOTS]], base=0, channel_multiplier=0,
                                   allow_small_or_imprecise_dtypes=True).then_inc(const_r, 1)
                    nc.gpsimd.memset(ones[:], 1.0).then_inc(const_r, 1)
                    nc.gpsimd.memset(tri[:], 1.0).then_inc(const_r, 1)
                    pool.wait_ge(const_r, 5)
                    nc.gpsimd.affine_select(out=tri[:], in_=tri[:], compare_op=ALU.is_gt, fill=0.0, base=0,
                                            pattern=[[1, P]], channel_multiplier=-1).then_inc(const_r, 1)
                    pool.wait_ge(pos_ready, 1)
                    for t in range(NT):
                        for k in range(2):
                            pool.indirect_dma_start(out=XS[:, :], out_offset=bass.IndirectOffsetOnAxis(
                                ap=posu[:, k, t:t + 1], axis=0), in_=XN[:, t, :], in_offset=None).then_inc(scattered, 16)
                    pool.wait_ge(scattered, 16 * 2 * NT)

                @block.tensor
                def _(pe):
                    pe.wait_ge(rw_loaded, 16)
                    for t in range(NT):
                        last = nc.tensor.matmul(LG[:, t * E:(t + 1) * E], XNT[:, t * P:(t + 1) * P], RW[:],
                                                start=True, stop=True)
                    last.then_inc(lg_done, 1)
                    pe.wait_ge(const_r, 6)
                    pe.wait_ge(m_ready, 1)
                    Mf = M[:].rearrange("p t e -> p (t e)")
                    nc.tensor.matmul(RC[:, 0].rearrange("p t e -> p (t e)"), tri[:], Mf, start=True, stop=True)
                    nc.tensor.matmul(RC[:, 1].rearrange("p t e -> p (t e)"), ones[:], Mf, start=True, stop=True)\
                      .then_inc(rc_done, 1)

                @block.scalar
                def _(act):
                    act.wait_ge(z_ready, 1)
                    nc.scalar.activation(ex[:], z[:], ACT.Exp).then_inc(ex_ready, 1)

                @block.vector
                def _(dve):
                    chain = Chain(dve, r_step)

                    def per_tile(ap):
                        return ap.unsqueeze(2).to_broadcast([P, NT, E])

                    lg = LG[:, 0:NT * E].rearrange("p (t e) -> p t e", e=E)
                    dve.wait_ge(lg_done, 1)
                    chain.link(nc.vector.reduce_max(lmax[:], lg, AX.X))
                    nc.vector.tensor_tensor(z[:], lg, per_tile(lmax[:]), ALU.subtract).then_inc(z_ready, 1)
                    dve.wait_ge(ex_ready, 1)
                    chain.link(nc.vector.reduce_sum(lsum[:], ex[:], AX.X))
                    chain.link(nc.vector.reciprocal(lrec[:], lsum[:]))
                    chain.link(nc.vector.tensor_tensor(prob[:], ex[:], per_tile(lrec[:]), ALU.mult))
                    for t in range(NT):
                        last = nc.vector.max(top[:, t, :], prob[:, t, :])
                    chain.link(last)
                    for t in range(NT):
                        last = nc.vector.max_index(tid[:, t, :], top[:, t, :], prob[:, t, :])
                    nc.vector.tensor_tensor(wsum[:], top[:, :, 0], top[:, :, 1], ALU.add)
                    chain.link(last)
                    chain.link(nc.vector.tensor_copy(tidf[:], tid[:, :, 0:2].rearrange("p t k -> p k t")))
                    chain.link(nc.vector.reciprocal(wrec[:], wsum[:]))
                    for k in range(2):
                        nc.vector.tensor_tensor(wts[:, k], top[:, :, k], wrec[:], ALU.mult)
                    dve.wait_ge(const_r, 6)
                    for k in range(2):
                        last = nc.vector.tensor_tensor(OH[:, k], ioe[:].unsqueeze(1).to_broadcast([P, NT, E]),
                                                       per_tile(tidf[:, k]), ALU.is_equal)
                    chain.link(last)
                    nc.vector.tensor_tensor(M[:], OH[:, 0], OH[:, 1], ALU.add).then_inc(m_ready, 1)
                    dve.wait_ge(rc_done, 1)
                    chain.link(nc.vector.tensor_copy(cnt[:], RC[:, 1]))
                    for e in range(E):
                        last = nc.vector.tensor_tensor_scan(out=cinc[:, :, e], data0=ones[:, 0:NT], data1=cnt[:, :, e],
                                                            initial=0.0, op0=ALU.mult, op1=ALU.add)
                    chain.link(last)
                    chain.link(nc.vector.tensor_tensor(over[:], cinc[:, NT - 1, :].unsqueeze(2).to_broadcast([P, E, NT]),
                                                       iot[:].unsqueeze(1).to_broadcast([P, E, NT]), ALU.is_gt))
                    chain.link(nc.vector.reduce_sum(tiles[:], over[:], AX.X))
                    chain.link(nc.vector.tensor_tensor_scan(out=ends[:], data0=ones[:, 0:E], data1=tiles[:], initial=0.0,
                                                            op0=ALU.mult, op1=ALU.add))
                    chain.link(nc.vector.tensor_tensor(base[:], ends[:], tiles[:], ALU.subtract))
                    chain.link(nc.vector.tensor_scalar(base[:], base[:], float(P), None, ALU.mult))
                    chain.link(nc.vector.tensor_tensor(pos[:], cinc[:], cnt[:], ALU.subtract))
                    chain.link(nc.vector.tensor_tensor(pos[:], pos[:], RC[:, 0], ALU.add))
                    chain.link(nc.vector.tensor_tensor(pos[:], pos[:], base[:].unsqueeze(1).to_broadcast([P, NT, E]), ALU.add))
                    for k in range(2):
                        last = nc.vector.tensor_tensor(sel[:, k], pos[:], OH[:, k], ALU.mult)
                    chain.link(last)
                    chain.link(nc.vector.reduce_sum(posf[:], sel[:], AX.X))
                    nc.vector.tensor_copy(posu[:], posf[:]).then_inc(pos_ready, 1)
                    chain.link(nc.vector.tensor_tensor(sover[:], ios[:].unsqueeze(2).to_broadcast([1, SLOTS, E]),
                                                       ends[0:1, :].unsqueeze(1).to_broadcast([1, SLOTS, E]), ALU.is_ge))
                    chain.link(nc.vector.reduce_sum(sef[:], sover[:], AX.X))
                    nc.vector.tensor_scalar(etab[:], sef[:], float(E - 1), None, ALU.min)

        with ExitStack() as c2:
            def sb2(name, shape, dt=F32):
                return c2.enter_context(nc.sbuf_tensor(f"{tag}_{name}", shape, dt))

            def s2(name):
                return nc.alloc_semaphore(f"{tag}_{name}")

            xs = sb2("xs", [P, 2, P])
            xt = sb2("xt", [P, 2, P])
            gs = sb2("gs", [P, 2, FF])
            hs = sb2("hs", [P, 2, FF])
            ht = sb2("ht", [P, 2, FF])
            ys = sb2("ys", [P, 2, P])
            XT = c2.enter_context(nc.psum_tensor(f"{tag}_XT", [P, 512], F32))
            GP = c2.enter_context(nc.psum_tensor(f"{tag}_GP", [P, 2, FF], F32))
            UP = c2.enter_context(nc.psum_tensor(f"{tag}_UP", [P, 2, FF], F32))
            HT = c2.enter_context(nc.psum_tensor(f"{tag}_HT", [P, FF], F32))
            YP = c2.enter_context(nc.psum_tensor(f"{tag}_YP", [P, 512], F32))
            xs_loaded = [s2(f"xs_loaded{i}") for i in range(2)]
            ys_stored = [s2(f"ys_stored{i}") for i in range(2)]
            xt_done, xt_copied, g_done, u_done, silu_done, h_ready, ht_done, ht_copied, y_done, y_copied = map(
                s2, ("xt_done", "xt_copied", "g_done", "u_done", "silu_done", "h_ready", "ht_done", "ht_copied", "y_done",
                     "y_copied"))

            with nc.Block() as block:
                @block.sync
                def _(sp):
                    def load(s, b):
                        sp.wait_ge(xt_done, s - 1)
                        sp.dma_start(xs[:, b], XS[bass.ds(s * P, P), :]).then_inc(xs_loaded[b], 16)
                    for s in range(2):
                        sp.dma_start(xs[:, s], XS[s * P:(s + 1) * P, :]).then_inc(xs_loaded[s], 16)
                    over_pairs(sp, 2, SLOTS, load)

                @block.gpsimd
                def _(pool):
                    def store(s, b):
                        pool.wait_ge(y_copied, s + 1)
                        pool.dma_start(YS[bass.ds(s * P, P), :], ys[:, b]).then_inc(ys_stored[b], 16)
                    over_pairs(pool, 0, SLOTS, store)
                    pool.wait_ge(ys_stored[0], 16 * ((SLOTS + 1) // 2))
                    pool.wait_ge(ys_stored[1], 16 * (SLOTS // 2))

                @block.tensor
                def _(pe):
                    def x_turn(s, b):
                        pe.wait_ge(xs_loaded[b], ((s + 2 - b) // 2) * 16 if isinstance(s, int) else (s - b) * 8 + 16)
                        if from_(s, 1):
                            pe.wait_ge(xt_copied, s)
                        nc.tensor.transpose(XT[:, 0:P], xs[:, b], ident[:]).then_inc(xt_done, 1)

                    def expert(s):
                        return pe.value_load(etab[0:1, bass.ds(s, 1)], min_val=0, max_val=E - 1)

                    def up(s, b):
                        e = expert(s)
                        pe.wait_ge(xt_copied, s + 1)
                        nc.tensor.matmul(GP[:, b], xt[:, b], WG[:, bass.ds(e, 1), :].rearrange("p o f -> p (o f)"),
                                         start=True, stop=True).then_inc(g_done, 1)
                        nc.tensor.matmul(UP[:, b], xt[:, b], WU[:, bass.ds(e, 1), :].rearrange("p o f -> p (o f)"),
                                         start=True, stop=True).then_inc(u_done, 1)

                    def h_turn(s, b):
                        pe.wait_ge(h_ready, s + 1)
                        if from_(s, 1):
                            pe.wait_ge(ht_copied, s)
                        for j in range(FK):
                            last = nc.tensor.transpose(HT[:, j * P:(j + 1) * P], hs[:, b, j * P:(j + 1) * P], ident[:])
                        last.then_inc(ht_done, 1)

                    def down(s, b):
                        e = expert(s)
                        pe.wait_ge(ht_copied, s + 1)
                        if from_(s, 1):
                            pe.wait_ge(y_copied, s)
                        for j in range(FK):
                            last = nc.tensor.matmul(YP[:, 0:P], ht[:, b, j * P:(j + 1) * P],
                                                    WD[:, bass.ds(e, 1), j, :].rearrange("p o d -> p (o d)"),
                                                    start=(j == 0), stop=(j == FK - 1))
                        last.then_inc(y_done, 1)

                    pe.wait_ge(experts_loaded, 48)
                    x_turn(0, 0)
                    up(0, 0)
                    x_turn(1, 1)

                    def step(s, b):
                        up(s + 1, 1 - b)
                        h_turn(s, b)
                        x_turn(s + 2, b)
                        down(s - 1, 1 - b)
                    up(1, 1)
                    h_turn(0, 0)
                    x_turn(2, 0)
                    step(1, 1)
                    over_pairs(pe, 2, SLOTS - 2, step)
                    s = SLOTS - 2
                    up(s + 1, (s + 1) % 2)
                    h_turn(s, s % 2)
                    down(s - 1, (s - 1) % 2)
                    h_turn(s + 1, (s + 1) % 2)
                    down(s, s % 2)
                    down(s + 1, (s + 1) % 2)

                @block.scalar
                def _(act):
                    def x_copy(s, b):
                        act.wait_ge(xt_done, s + 1)
                        nc.scalar.activation(xt[:, b], XT[:, 0:P], ACT.Copy).then_inc(xt_copied, 1)

                    def silu(s, b):
                        act.wait_ge(g_done, s + 1)
                        nc.scalar.activation(gs[:, b], GP[:, b], ACT.Silu).then_inc(silu_done, 1)

                    def h_copy(s, b):
                        act.wait_ge(ht_done, s + 1)
                        nc.scalar.activation(ht[:, b], HT[:], ACT.Copy).then_inc(ht_copied, 1)

                    def body(s, b):
                        silu(s, b)
                        h_copy(s - 1, 1 - b)
                        x_copy(s + 1, 1 - b)
                    x_copy(0, 0)
                    silu(0, 0)
                    x_copy(1, 1)
                    over_pairs(act, 1, SLOTS - 1, body)
                    s = SLOTS - 1
                    silu(s, s % 2)
                    h_copy(s - 1, (s - 1) % 2)
                    h_copy(s, s % 2)

                @block.vector
                def _(dve):
                    def gate(s, b):
                        dve.wait_ge(silu_done, s + 1)
                        dve.wait_ge(u_done, s + 1)
                        nc.vector.tensor_tensor(hs[:, b], gs[:, b], UP[:, b], ALU.mult).then_inc(h_ready, 1)

                    def y_copy(s, b):
                        dve.wait_ge(y_done, s + 1)
                        if not isinstance(s, int) or s >= 2:
                            dve.wait_ge(ys_stored[b], (s - b) * 8)
                        nc.vector.tensor_copy(ys[:, b], YP[:, 0:P]).then_inc(y_copied, 1)

                    def body(s, b):
                        gate(s, b)
                        y_copy(s - 2, b)
                    gate(0, 0)
                    gate(1, 1)
                    body(2, 0)
                    body(3, 1)
                    over_pairs(dve, 4, SLOTS, body)
                    y_copy(SLOTS - 2, SLOTS % 2)
                    y_copy(SLOTS - 1, (SLOTS - 1) % 2)

        with ExitStack() as c2:
            GB = c2.enter_context(nc.sbuf_tensor(f"{tag}_GB", [P, NT, 2, P], F32))
            gathered = [nc.alloc_semaphore(f"{tag}_gathered{i}") for i in range(4)]
            added = nc.alloc_semaphore(f"{tag}_added")
            with nc.Block() as block:
                @block.gpsimd
                def _(pool):
                    for t in range(NT):
                        for k in range(2):
                            pool.indirect_dma_start(out=GB[:, t, k, :], out_offset=None, in_=YS[:, :],
                                                    in_offset=bass.IndirectOffsetOnAxis(ap=posu[:, k, t:t + 1], axis=0))\
                                .then_inc(gathered[t // 4], 16)

                @block.vector
                def _(dve):
                    for q in range(4):
                        dve.wait_ge(gathered[q], 16 * 8)
                        for k in range(2):
                            if k:
                                dve.wait_ge(added, 4 * (2 * q + 1))
                            for t in range(4 * q, 4 * q + 4):
                                nc.vector.scalar_tensor_tensor(out=X[:, t, :], in0=GB[:, t, k, :], scalar=wts[:, k, t:t + 1],
                                                               in1=X[:, t, :], op0=ALU.mult, op1=ALU.add).then_inc(added, 1)


def decay_attention(nc, X, ident, identb, io):
    NT, CPS, D, H, DH = 16, 8, 128, 16, 64
    HP, HG = H // 2, 4
    VW = DH + 1
    EPS, SHIFT = 1e-6, 2.0

    with ExitStack() as ctx:
        def sb(name, shape, dt=F32):
            return ctx.enter_context(nc.sbuf_tensor("d_" + name, shape, dt))

        def sem(name):
            return nc.alloc_semaphore("d_" + name)

        XNT = sb("XNT", [P, NT * P])
        WQ, WK, WV = (sb(n, [P, H * DH]) for n in ("WQ", "WK", "WV"))
        WO = sb("WO", [P, HP, D])
        WA = sb("WA", [P, H])
        ba = sb("ba", [P, H])
        triu = sb("triu", [P, P])
        later = sb("later", [P, P], BF16)
        LT = sb("LT", [3 * H, NT, P], BF16)
        pick = sb("pick", [3 * H, H, P], BF16)
        ones = sb("ones", [P, P])
        la, L, nL, eL, wk, rem = (sb(n, [P, NT, H]) for n in ("la", "L", "nL", "eL", "wk", "rem"))
        dec = sb("dec", [P, NT, HP])
        S = sb("S", [P, HP, 2, VW])
        V1 = sb("V1", [P, 2, H, VW])
        wb_loaded = sem("w_loaded")
        with ExitStack() as c2:
            XN = c2.enter_context(nc.sbuf_tensor("d_XN", [P, NT, P], F32))
            with nc.Block() as blk:
                @blk.sync
                def _(sp):
                    for w, n in ((WA, "Wa"), (WK, "Wk"), (WV, "Wv"), (WQ, "Wq")):
                        sp.dma_start(w[:], io[n]).then_inc(wb_loaded, 16)
                    sp.dma_start(ba[:], io["ba"].partition_broadcast(P)).then_inc(wb_loaded, 16)
                    sp.dma_start(WO[:], io["Wo"].rearrange("(k p) d -> p k d", p=P)).then_inc(wb_loaded, 16)
            layer_norm(nc, "d_ln", X, XN, XNT, ident, NT)

        with ExitStack() as c2:
            zz, mz, ez, lz = (c2.enter_context(nc.sbuf_tensor("d_" + n, [P, NT, H], F32)) for n in ("zz", "mz", "ez", "lz"))
            ZP = c2.enter_context(nc.psum_tensor("d_ZP", [P, 512], F32))
            LP = c2.enter_context(nc.psum_tensor("d_LP", [P, 512], F32))
            TP = c2.enter_context(nc.psum_tensor("d_TP", [P, 512], F32))
            LTP = c2.enter_context(nc.psum_tensor("d_LTP", [3 * H, NT // 4, 512], F32))
            Lp = c2.enter_context(nc.sbuf_tensor("d_Lp", [P, NT, 3, H], BF16))
            Lr = c2.enter_context(nc.sbuf_tensor("d_Lr", [P, NT, H], F32))
            const_d, z_done, step, mz_ready, ez_ready, ez1_ready, lz_ready, la_ready, l_done, rem_ready, l_ready, e_ready, lp_ready, lt_done = map(
                lambda n: nc.alloc_semaphore("d_" + n),
                ("const", "z_done", "step", "mz_ready", "ez_ready", "ez1_ready", "lz_ready", "la_ready", "l_done",
                 "rem_ready", "l_ready", "e_ready", "lp_ready", "lt_done"))
            with nc.Block() as block:
                @block.gpsimd
                def _(pool):
                    nc.gpsimd.memset(ones[:], 1.0).then_inc(const_d, 1)
                    nc.gpsimd.memset(triu[:], 1.0).then_inc(const_d, 1)
                    pool.wait_ge(const_d, 2)
                    nc.gpsimd.affine_select(out=triu[:], in_=triu[:], compare_op=ALU.is_ge, fill=0.0, base=0,
                                            pattern=[[1, P]], channel_multiplier=-1).then_inc(const_d, 1)
                    nc.gpsimd.memset(later[:], 0.0).then_inc(const_d, 1)
                    pool.wait_ge(const_d, 4)
                    nc.gpsimd.affine_select(out=later[:], in_=later[:], compare_op=ALU.is_ge, fill=NEG, base=0,
                                            pattern=[[1, P]], channel_multiplier=-1).then_inc(const_d, 1)
                    nc.gpsimd.memset(S[:], 0.0).then_inc(const_d, 1)
                    nc.gpsimd.memset(V1[:], 1.0).then_inc(const_d, 1)
                    nc.gpsimd.memset(pick[:], 0.0).then_inc(const_d, 1)
                    for part in range(3):
                        pool.wait_ge(const_d, 8 + part)
                        nc.gpsimd.affine_select(out=pick[:], in_=pick[:], compare_op=ALU.not_equal, fill=1.0,
                                                base=-H * part, pattern=[[-1, H], [0, P]],
                                                channel_multiplier=1).then_inc(const_d, 1)

                @block.tensor
                def _(pe):
                    pe.wait_ge(wb_loaded, 16 * 6)
                    for t in range(NT):
                        last = nc.tensor.matmul(ZP[:, t * H:(t + 1) * H], XNT[:, t * P:(t + 1) * P], WA[:],
                                                start=True, stop=True)
                    last.then_inc(z_done, 1)
                    pe.wait_ge(const_d, 7)
                    pe.wait_ge(la_ready, 1)
                    laf = la[:].rearrange("p t h -> p (t h)")
                    nc.tensor.matmul(LP[:, 0:NT * H], triu[:], laf, start=True, stop=True)
                    nc.tensor.matmul(TP[:, 0:NT * H], ones[:], laf, start=True, stop=True).then_inc(l_done, 1)
                    pe.wait_ge(lp_ready, 1)
                    for t in range(NT):
                        nc.tensor.matmul(LTP[:, t // 4, (t % 4) * P:(t % 4 + 1) * P],
                                         Lp[:, t].rearrange("p a h -> p (a h)"), identb[:],
                                         start=True, stop=True).then_inc(lt_done, 1)

                @block.scalar
                def _(act):
                    act.wait_ge(mz_ready, 1)
                    nc.scalar.activation(ez[:], mz[:], ACT.Exp).then_inc(ez_ready, 1)
                    act.wait_ge(ez1_ready, 1)
                    nc.scalar.activation(lz[:], ez[:], ACT.Ln).then_inc(lz_ready, 1)
                    act.wait_ge(l_ready, 1)
                    nc.scalar.activation(eL[:], L[:], ACT.Exp).then_inc(e_ready, 1)
                    act.wait_ge(rem_ready, 1)
                    nc.scalar.activation(wk[:], rem[:], ACT.Exp).then_inc(e_ready, 1)
                    tp = TP[:, 0:NT * H].rearrange("p (t k h) -> p t k h", t=NT, h=2)
                    for h in range(2):
                        q = slice(64 * h, 64 * h + 64)
                        nc.scalar.activation(dec[q], tp[q, :, :, h], ACT.Exp).then_inc(e_ready, 1)
                    for q in range(NT // 4):
                        act.wait_ge(lt_done, 4 * q + 4)
                        nc.scalar.activation(LT[:, 4 * q:4 * q + 4].rearrange("p t n -> p (t n)"), LTP[:, q], ACT.Copy)

                @block.vector
                def _(dve):
                    chain = Chain(dve, step)
                    dve.wait_ge(z_done, 1)
                    zp = ZP[:, 0:NT * H].rearrange("p (t h) -> p t h", h=H)
                    chain.link(nc.vector.tensor_tensor(zz[:], zp, ba[:].unsqueeze(1).to_broadcast([P, NT, H]), ALU.add))
                    chain.link(nc.vector.tensor_scalar_add(zz[:], zz[:], SHIFT))
                    nc.vector.scalar_tensor_tensor(out=mz[:], in0=zz[:], scalar=-1.0, in1=zz[:], op0=ALU.mult,
                                                   op1=ALU.min).then_inc(mz_ready, 1)
                    dve.wait_ge(ez_ready, 1)
                    nc.vector.tensor_scalar_add(ez[:], ez[:], 1.0).then_inc(ez1_ready, 1)
                    dve.wait_ge(lz_ready, 1)
                    nc.vector.scalar_tensor_tensor(out=la[:], in0=zz[:], scalar=0.0, in1=lz[:], op0=ALU.min,
                                                   op1=ALU.subtract).then_inc(la_ready, 1)
                    dve.wait_ge(l_done, 1)
                    nc.vector.tensor_copy(L[:].rearrange("p t h -> p (t h)"), LP[:, 0:NT * H]).then_inc(l_ready, 1)
                    dve.wait_ge(l_ready, 1)
                    nc.vector.tensor_tensor(rem[:].rearrange("p t h -> p (t h)"), TP[:, 0:NT * H],
                                            L[:].rearrange("p t h -> p (t h)"), ALU.subtract).then_inc(rem_ready, 1)
                    nc.vector.tensor_scalar_mul(nL[:], L[:], -1.0)
                    chain.link(nc.vector.tensor_copy(Lp[:, :, 0], L[:]))
                    chain.link(nc.vector.tensor_tensor(Lr[:], L[:], Lp[:, :, 0], ALU.subtract))
                    chain.link(nc.vector.tensor_copy(Lp[:, :, 1], Lr[:]))
                    nc.vector.tensor_tensor(Lp[:, :, 2], Lr[:], Lp[:, :, 1], ALU.subtract).then_inc(lp_ready, 1)
                    dve.wait_ge(e_ready, 4)
                    for t in range(0, NT, CPS):
                        nc.vector.memset(eL[:, t, :], 0.0)
                        nc.vector.memset(dec[:, t, :], 0.0)

        xc = sb("xc", [P, 2, P])
        nlc = sb("nlc", [P, 2, H])
        etmp = sb("etmp", [P, 4, 512])
        enegs = sb("enegs", [P, 4, 512])
        Kn = sb("Kn", [P, 2, H * DH])
        QT = sb("QT", [P, 2, HP, P])
        KTZ = sb("KTZ", [P, 2, HP, 2, P])
        KS = sb("KS", [P, 2, H * DH])
        SD = sb("SD", [P, HP, 2, VW])
        DM = sb("DM", [P, 2, 4, P])
        WB = sb("WB", [P, 2, 4, P])
        ox = sb("ox", [P, 4, VW])
        O = sb("O", [P, 2, H, VW])
        rd = sb("rd", [P, H])
        YN = sb("YN", [P, H * DH])
        YTS = sb("YTS", [P, HP, P])

        def psum(name, shape):
            return ctx.enter_context(nc.psum_tensor("d_" + name, shape, F32))

        PA, AT, LB = psum("PA", [P, 2, 512]), psum("AT", [P, 4, P]), psum("LB", [P, 4, P])
        OI, OX = psum("OI", [P, 512]), psum("OX", [P, 512])
        TR, SU = psum("TR", [P, 4, P]), psum("SU", [P, 512])
        names = ("ktz_zero", "xc_ready", "proj_done", "elu_done", "v_done", "exp_done", "yt_done", "yt_copied", "kt_done",
                 "kt_copied", "lb_done", "at_done", "expd_done", "neg_done", "w_done", "inter_done", "intra_done",
                 "ox_ready", "comb_done", "rd_step", "rd_ready", "yn_done", "wo_done", "x_added", "su_done", "ks_done",
                 "sd_done", "supd_done")
        (ktz_zero, xc_ready, proj_done, elu_done, v_done, exp_done, yt_done, yt_copied, kt_done,
         kt_copied, lb_done, at_done, expd_done, neg_done, w_done, inter_done, intra_done,
         ox_ready, comb_done, rd_step, rd_ready, yn_done, wo_done, x_added, su_done, ks_done,
         sd_done, supd_done) = map(sem, names)

        with nc.Block() as block:
            @block.tensor
            def _(pe):
                def project_natural(b, bank, W, c):
                    nc.tensor.matmul(PA[:, bank, :], xc[:, b], W[:, c * 512:(c + 1) * 512], start=True, stop=True)\
                      .then_inc(proj_done, 1)

                def keys(n, b):
                    pe.wait_ge(xc_ready, n + 1)
                    for c in range(2):
                        if from_(n, 1):
                            pe.wait_ge(elu_done, n * 4 + (c - 1))
                        project_natural(b, c, WK, c)

                def values(n, b, c):
                    pe.wait_ge(elu_done, n * 4 + (c + 1))
                    project_natural(b, c, WV, c)

                def queries(n, b, c):
                    pe.wait_ge(v_done, n * 2 + (c + 1))
                    for j in range(4):
                        hp = 4 * c + j
                        last = nc.tensor.matmul(PA[:, c, j * P:(j + 1) * P], WQ[:, hp * P:(hp + 1) * P], xc[:, b],
                                                start=True, stop=True)
                    last.then_inc(proj_done, 1)

                def keys_turn(n, b, c):
                    if c:
                        pe.wait_ge(kt_copied, n * 2 + 1)
                    else:
                        pe.wait_ge(elu_done, n * 4 + 2)
                        if from_(n, 2):
                            pe.wait_ge(yt_copied, (n - 1) * 2)
                        elif n == 1:
                            pe.wait_ge(kt_copied, 2)
                    for j in range(4):
                        hp = 4 * c + j
                        last = nc.tensor.transpose(TR[:, j], Kn[:, b, hp * P:(hp + 1) * P], ident[:])
                    last.then_inc(kt_done, 1)

                def outputs_turn(t, c):
                    if c:
                        pe.wait_ge(yt_copied, t * 2 + 1)
                    else:
                        pe.wait_ge(yn_done, t + 1)
                        pe.wait_ge(kt_copied, t * 2 + 4 if not isinstance(t, int) or t < NT - 1 else 2 * NT)
                    for j in range(4):
                        hp = 4 * c + j
                        last = nc.tensor.transpose(TR[:, j], YN[:, hp * P:(hp + 1) * P], ident[:])
                    last.then_inc(yt_done, 1)

                def project_out(t, half_updates):
                    pe.wait_ge(yt_copied, t * 2 + 2)
                    pe.wait_ge(supd_done, half_updates)
                    for hp in range(HP):
                        last = nc.tensor.matmul(SU[:, 0:D], YTS[:, hp], WO[:, hp], start=(hp == 0), stop=(hp == HP - 1))
                    last.then_inc(wo_done, 1)

                def decays(t, b, i):
                    if i or from_(t, 1):
                        pe.wait_ge(expd_done, t * 4 + i)
                    nc.tensor.matmul(LB[:], identb[:], later[:].unsqueeze(1).to_broadcast([P, 4, P]),
                                     start=True, stop=False)
                    for j in range(4):
                        last = nc.tensor.matmul(LB[:, j], pick[:, 4 * i + j],
                                                LT[:, bass.ds(t, 1), :].rearrange("p o n -> p (o n)"),
                                                start=False, stop=(j == 3))
                    last.then_inc(lb_done, 1)

                def scores(t, b, i):
                    if i or from_(t, 1):
                        pe.wait_ge(w_done, t * 4 + i)
                    if i % 2 == 0:
                        pe.wait_ge(kt_copied, t * 2 + (1 + i // 2))
                        pe.wait_ge(elu_done, t * 4 + (3 + i // 2))
                    for j in range(4):
                        h = 4 * i + j
                        last = nc.tensor.matmul(AT[:, j], KTZ[:, b, h // 2, h % 2, :], QT[:, b, h // 2, :],
                                                start=True, stop=True)
                    last.then_inc(at_done, 1)

                def across_chunks(t, b, i):
                    if i or from_(t, 1):
                        pe.wait_ge(comb_done, t * 4 + i)
                    if from_(t, 1) and i % 2 == 0:
                        pe.wait_ge(supd_done, t * 2 + (i // 2 - 1))
                    for j in range(2):
                        hp = 2 * i + j
                        last = nc.tensor.matmul(OX[:, 2 * j * VW:2 * (j + 1) * VW], QT[:, b, hp, :],
                                                S[:, hp].rearrange("p h v -> p (h v)"), start=True, stop=True)
                    last.then_inc(inter_done, 1)

                def within_chunk(t, b, i):
                    pe.wait_ge(w_done, t * 4 + (i + 1))
                    for j in range(4):
                        h = 4 * i + j
                        last = nc.tensor.matmul(OI[:, j * VW:(j + 1) * VW], WB[:, i % 2, j, :], V1[:, b, h, :],
                                                start=True, stop=True)
                    last.then_inc(intra_done, 1)

                def state(t, b, c):
                    if c == 0:
                        pe.wait_ge(ks_done, t + 1)
                        if from_(t, 1):
                            pe.wait_ge(supd_done, t * 2)
                    elif from_(t, 1):
                        pe.wait_ge(x_added, t)
                    else:
                        pe.wait_ge(supd_done, 1)
                    for j in range(4):
                        for h in range(2):
                            hh = 2 * (4 * c + j) + h
                            last = nc.tensor.matmul(SU[64 * h:64 * h + 64, j * VW:(j + 1) * VW],
                                                    KS[:, b, hh * DH:(hh + 1) * DH], V1[:, b, hh, :],
                                                    start=True, stop=True)
                    last.then_inc(su_done, 1)

                def slot(t, b, i, last=False):
                    if i < 3:
                        decays(t, b, i + 1)
                    elif not last:
                        decays(t + 1, 1 - b, 0)
                    across_chunks(t, b, i)
                    within_chunk(t, b, i)
                    if i < 3:
                        scores(t, b, i + 1)
                    elif not last:
                        scores(t + 1, 1 - b, 0)

                def step(t, b, last=False):
                    first = isinstance(t, int) and t == 0
                    n, nb = t + 1, 1 - b
                    slot(t, b, 0)
                    if not first:
                        state(t - 1, nb, 1)
                    if not last:
                        keys(n, nb)
                    slot(t, b, 1)
                    state(t, b, 0)
                    for c in range(2):
                        if not last:
                            values(n, nb, c)
                        if not first:
                            outputs_turn(t - 1, c)
                    slot(t, b, 2)
                    for c in range(2):
                        if not last:
                            keys_turn(n, nb, c)
                            queries(n, nb, c)
                    slot(t, b, 3, last)
                    if not first:
                        project_out(t - 1, t * 2 + 1)

                pe.wait_ge(ktz_zero, 1)
                keys(0, 0)
                for c in range(2):
                    values(0, 0, c)
                for c in range(2):
                    keys_turn(0, 0, c)
                    queries(0, 0, c)
                decays(0, 0, 0)
                scores(0, 0, 0)
                step(0, 0)
                step(1, 1)
                over_pairs(pe, 2, NT - 1, step)
                step(NT - 1, (NT - 1) % 2, last=True)
                for c in range(2):
                    outputs_turn(NT - 1, c)
                pe.wait_ge(x_added, NT - 1)
                project_out(NT - 1, 2 * NT - 1)

            @block.scalar
            def _(act):
                def exp_(n, k, j):
                    act.wait_ge(proj_done, n * 6 + (j + 1))
                    if from_(n, 1):
                        act.wait_ge(elu_done, n * 4 + (k - 3))
                    nc.scalar.activation(enegs[:, k], PA[:, j % 2], ACT.Relu, scale=-1.0).then_inc(neg_done, 1)
                    act.wait_ge(neg_done, n * 4 + (k + 1))
                    nc.scalar.activation(etmp[:, k], enegs[:, k], ACT.Exp, scale=-1.0).then_inc(exp_done, 1)

                def v_copy(n, b, c):
                    act.wait_ge(proj_done, n * 6 + (3 + c))
                    if from_(n, 2):
                        act.wait_ge(intra_done, (n - 1) * 4)
                        act.wait_ge(su_done, (n - 1) * 2)
                    nc.scalar.activation(V1[:, b, 8 * c:8 * c + 8, 0:DH], PA[:, c].rearrange("p (h v) -> p h v", v=DH),
                                         ACT.Copy).then_inc(v_done, 1)

                def kt_copy(n, b, c):
                    act.wait_ge(kt_done, n * 2 + (c + 1))
                    if from_(n, 2):
                        act.wait_ge(at_done, (n - 1) * 4)
                    for h in range(2):
                        q = slice(64 * h, 64 * h + 64)
                        last = nc.scalar.activation(KTZ[q, b, 4 * c:4 * c + 4, h, :], TR[q], ACT.Copy)
                    last.then_inc(kt_copied, 1)

                def yt_copy(t, c):
                    act.wait_ge(yt_done, t * 2 + (c + 1))
                    if from_(t, 1):
                        act.wait_ge(wo_done, t)
                    nc.scalar.activation(YTS[:, 4 * c:4 * c + 4], TR[:], ACT.Copy).then_inc(yt_copied, 1)

                def exp_decay(t, b, i):
                    act.wait_ge(lb_done, t * 4 + (i + 1))
                    if i == 0:
                        act.wait_ge(xc_ready, t + 1)
                    if i >= 2 or from_(t, 1):
                        act.wait_ge(w_done, t * 4 + (i - 1))
                    for j in range(4):
                        h = 4 * i + j
                        last = nc.scalar.activation(DM[:, i % 2, j], LB[:, j], ACT.Exp, bias=nlc[:, b, h:h + 1])
                    last.then_inc(expd_done, 1)

                def step(t, b, last=False):
                    first = isinstance(t, int) and t == 0
                    n, nb = t + 1, 1 - b
                    exp_decay(t, b, 1)
                    if not last:
                        exp_(n, 0, 0)
                        exp_(n, 1, 1)
                    exp_decay(t, b, 2)
                    for c in range(2):
                        if not last:
                            v_copy(n, nb, c)
                        if not first:
                            yt_copy(t - 1, c)
                    exp_decay(t, b, 3)
                    if not last:
                        for c in range(2):
                            kt_copy(n, nb, c)
                            exp_(n, 2 + c, 4 + c)
                        exp_decay(n, nb, 0)

                act.wait_ge(ktz_zero, 1)
                exp_(0, 0, 0)
                exp_(0, 1, 1)
                v_copy(0, 0, 0)
                v_copy(0, 0, 1)
                for c in range(2):
                    kt_copy(0, 0, c)
                    exp_(0, 2 + c, 4 + c)
                exp_decay(0, 0, 0)
                step(0, 0)
                step(1, 1)
                over_pairs(act, 2, NT - 1, step)
                step(NT - 1, (NT - 1) % 2, last=True)
                yt_copy(NT - 1, 0)
                yt_copy(NT - 1, 1)

            @block.gpsimd
            def _(pool):
                def x_copy(n, b):
                    if from_(n, 2):
                        pool.wait_ge(proj_done, (n - 1) * 6)
                        pool.wait_ge(expd_done, (n - 1) * 4)
                    nc.gpsimd.tensor_copy(xc[:, b], XNT[:, bass.ds(n * P, P)])
                    nc.gpsimd.tensor_copy(nlc[:, b], nL[:, bass.ds(n, 1), :].rearrange("p o h -> p (o h)"))\
                      .then_inc(xc_ready, 1)

                def keys_decayed(t, b):
                    pool.wait_ge(elu_done, t * 4 + 2)
                    if from_(t, 2):
                        pool.wait_ge(su_done, (t - 1) * 2)
                    nc.gpsimd.tensor_tensor(KS[:, b].rearrange("p (h v) -> p h v", v=DH),
                                            Kn[:, b].rearrange("p (h v) -> p h v", v=DH),
                                            wk[:, bass.ds(t, 1), :].rearrange("p o h -> p (o h)").unsqueeze(2)
                                            .to_broadcast([P, H, DH]), ALU.mult).then_inc(ks_done, 1)

                def state_decayed(t, c):
                    if from_(t, 1):
                        pool.wait_ge(supd_done, t * 2 + (c - 1))
                    q = slice(4 * c, 4 * c + 4)
                    nc.gpsimd.tensor_tensor(SD[:, q].rearrange("p k h v -> p k (h v)"),
                                            S[:, q].rearrange("p k h v -> p k (h v)"),
                                            dec[:, bass.ds(t, 1), q].rearrange("p o h -> p (o h)").unsqueeze(2)
                                            .to_broadcast([P, 4, 2 * VW]), ALU.mult).then_inc(sd_done, 1)

                def divide(t, b):
                    pool.wait_ge(rd_ready, t + 1)
                    if from_(t, 1):
                        pool.wait_ge(yt_done, t * 2)
                    nc.gpsimd.tensor_tensor(YN[:].rearrange("p (h v) -> p h v", v=DH), O[:, b, :, 0:DH],
                                            rd[:].unsqueeze(2).to_broadcast([P, H, DH]), ALU.mult).then_inc(yn_done, 1)

                def step(t, b, last=False, copy=True):
                    first = isinstance(t, int) and t == 0
                    if not first:
                        divide(t - 1, 1 - b)
                    state_decayed(t, 1)
                    if not last:
                        keys_decayed(t + 1, 1 - b)
                        state_decayed(t + 1, 0)
                    if copy:
                        x_copy(t + 2, b)

                nc.gpsimd.memset(KTZ[:], 0.0).then_inc(ktz_zero, 1)
                x_copy(0, 0)
                x_copy(1, 1)
                state_decayed(0, 0)
                keys_decayed(0, 0)
                step(0, 0)
                step(1, 1)
                over_pairs(pool, 2, NT - 2, step)
                step(NT - 2, (NT - 2) % 2, copy=False)
                step(NT - 1, (NT - 1) % 2, last=True, copy=False)
                divide(NT - 1, (NT - 1) % 2)

            @block.vector
            def _(dve):
                def elu(n, k, j, dst):
                    dve.wait_ge(exp_done, n * 4 + (k + 1))
                    nc.vector.scalar_tensor_tensor(out=dst, in0=PA[:, j % 2], scalar=0.0, in1=etmp[:, k], op0=ALU.max,
                                                   op1=ALU.add).then_inc(elu_done, 1)

                def elu_keys(n, b):
                    if from_(n, 2):
                        dve.wait_ge(kt_done, (n - 1) * 2)
                        dve.wait_ge(ks_done, n - 1)
                    for c in range(2):
                        elu(n, c, c, Kn[:, b, c * 512:(c + 1) * 512])

                def elu_queries(n, b):
                    if from_(n, 2):
                        dve.wait_ge(inter_done, (n - 1) * 4)
                    for c in range(2):
                        elu(n, 2 + c, 4 + c, QT[:, b, 4 * c:4 * c + 4].rearrange("p k q -> p (k q)"))

                def weigh(t, i):
                    dve.wait_ge(expd_done, t * 4 + (i + 1))
                    dve.wait_ge(at_done, t * 4 + (i + 1))
                    if i >= 2 or from_(t, 1):
                        dve.wait_ge(intra_done, t * 4 + (i - 1))
                    nc.vector.tensor_tensor(WB[:, i % 2], AT[:], DM[:, i % 2], ALU.mult).then_inc(w_done, 1)

                def combine(t, b, i):
                    dve.wait_ge(intra_done, t * 4 + (i + 1))
                    if i == 0 and from_(t, 2):
                        dve.wait_ge(yn_done, t - 1)
                    nc.vector.tensor_tensor(ox[:], OX[:, 0:4 * VW].rearrange("p (h v) -> p h v", v=VW),
                                            eL[:, bass.ds(t, 1), 4 * i:4 * i + 4].rearrange("p o h -> p (o h)")
                                            .unsqueeze(2).to_broadcast([P, 4, VW]), ALU.mult).then_inc(ox_ready, 1)
                    dve.wait_ge(ox_ready, t * 4 + (i + 1))
                    nc.vector.tensor_tensor(O[:, b, 4 * i:4 * i + 4].rearrange("p h v -> p (h v)"), OI[:, 0:4 * VW],
                                            ox[:].rearrange("p h v -> p (h v)"), ALU.add).then_inc(comb_done, 1)

                def reciprocals(t, b):
                    dve.wait_ge(comb_done, t * 4 + 4)
                    if from_(t, 1):
                        dve.wait_ge(yn_done, t)
                    nc.vector.tensor_scalar_add(rd[:], O[:, b, :, DH], EPS).then_inc(rd_step, 1)
                    dve.wait_ge(rd_step, t + 1)
                    nc.vector.reciprocal(rd[:], rd[:]).then_inc(rd_ready, 1)

                def update(t, c):
                    dve.wait_ge(su_done, t * 2 + (c + 1))
                    dve.wait_ge(sd_done, t * 2 + (c + 1))
                    dve.wait_ge(inter_done, t * 4 + (2 * c + 2))
                    for h in range(2):
                        q = slice(64 * h, 64 * h + 64)
                        last = nc.vector.tensor_tensor(S[q, 4 * c:4 * c + 4, h, :],
                                                       SU[q, 0:4 * VW].rearrange("p (k v) -> p k v", v=VW),
                                                       SD[q, 4 * c:4 * c + 4, h, :], ALU.add)
                    last.then_inc(supd_done, 1)

                def add_out(t):
                    dve.wait_ge(wo_done, t + 1)
                    xs = X[:, bass.ds(t, 1), :].rearrange("p o d -> p (o d)")
                    nc.vector.tensor_tensor(xs, xs, SU[:, 0:D], ALU.add).then_inc(x_added, 1)

                def step(t, b, last=False):
                    first = isinstance(t, int) and t == 0
                    n, nb = t + 1, 1 - b
                    combine(t, b, 0)
                    weigh(t, 1)
                    if not first:
                        update(t - 1, 1)
                    if not last:
                        elu_keys(n, nb)
                    combine(t, b, 1)
                    weigh(t, 2)
                    update(t, 0)
                    combine(t, b, 2)
                    weigh(t, 3)
                    if not last:
                        elu_queries(n, nb)
                    combine(t, b, 3)
                    reciprocals(t, b)
                    if not last:
                        weigh(n, 0)
                    if not first:
                        add_out(t - 1)

                elu_keys(0, 0)
                elu_queries(0, 0)
                weigh(0, 0)
                step(0, 0)
                step(1, 1)
                over_pairs(dve, 2, NT - 1, step)
                step(NT - 1, (NT - 1) % 2, last=True)
                add_out(NT - 1)


def program(nc, io, out, upto="all"):
    NT = 16
    with ExitStack() as ctx:
        X = ctx.enter_context(nc.sbuf_tensor("X", [P, NT, P], F32))
        W3 = ctx.enter_context(nc.sbuf_tensor("W3", [P, 3 * Router.E * Router.FF], F32))
        experts_loaded = ctx.enter_context(nc.semaphore("experts_loaded"))
        zeros_stored = ctx.enter_context(nc.semaphore("zeros_stored"))
        ident = ctx.enter_context(nc.sbuf_tensor("ident", [P, P], F32))
        identb = ctx.enter_context(nc.sbuf_tensor("identb", [P, P], BF16))
        zeros_ready = ctx.enter_context(nc.semaphore("zeros_ready"))
        ident_zero = ctx.enter_context(nc.semaphore("ident_zero"))
        out_stored = ctx.enter_context(nc.semaphore("out_stored"))
        scratch = {"qk": nc.dram_tensor("qk_parts", [2, 3, 16, 2, 2, 8, 1024], BF16, kind="Internal"),
                   "xs": nc.dram_tensor("xs_rows", [Router.SLOTS * P, P], F32, kind="Internal"),
                   "ys": nc.dram_tensor("ys_rows", [Router.SLOTS * P, P], F32, kind="Internal")}
        with nc.Block() as block:
            @block.gpsimd
            def _(pool):
                nc.gpsimd.memset(ident[:], 0.0).then_inc(ident_zero, 1)
                nc.gpsimd.memset(identb[:], 0.0).then_inc(ident_zero, 1)
                pool.wait_ge(ident_zero, 2)
                for m in (ident, identb):
                    nc.gpsimd.affine_select(out=m[:], in_=m[:], compare_op=ALU.not_equal, fill=1.0, base=0,
                                            pattern=[[-1, P]], channel_multiplier=1).then_inc(ident_zero, 1)
            @block.vector
            def _(dve):
                nc.vector.memset(W3[:, 0:Router.SLOTS * P], 0.0).then_inc(zeros_ready, 1)

            @block.sync
            def _(sp):
                sp.wait_ge(zeros_ready, 1)
                sp.dma_start(scratch["xs"][:, :].rearrange("(s p) d -> p s d", p=P),
                             W3[:, 0:Router.SLOTS * P].rearrange("p (s d) -> p s d", d=P)).then_inc(zeros_stored, 16)
                sp.wait_ge(zeros_stored, 16)
        a = {n[len("L0_attn_a_"):]: ap for n, ap in io.items() if n.startswith("L0_attn_a_")}
        f = {n[len("L0_ffn_"):]: ap for n, ap in io.items() if n.startswith("L0_ffn_")}
        with nc.cleanup_on_exit():
            diff_attention(nc, X, W3, ident, identb, a, scratch,
                           lambda sp: load_experts(nc, sp, W3, f, experts_loaded))
        if upto != "attn_a":
            with nc.cleanup_on_exit():
                moe(nc, "m1", X, W3, ident, f, scratch, experts_loaded)
        if upto not in ("attn_a", "ffn1"):
            d = {n[len("L0_attn_b_"):]: ap for n, ap in io.items() if n.startswith("L0_attn_b_")}
            with nc.cleanup_on_exit():
                decay_attention(nc, X, ident, identb, d)
        if upto == "all":
            with nc.cleanup_on_exit():
                moe(nc, "m2", X, W3, ident, f, scratch, experts_loaded)
        with nc.Block() as block:
            @block.sync
            def _(sp):
                sp.dma_start(out.rearrange("b (t p) d -> p (b t) d", p=P), X[:]).then_inc(out_stored, 16)
                sp.wait_ge(out_stored, 16)


_INS = ["L0_attn_a_x", "L0_attn_a_Wq1", "L0_attn_a_Wq2", "L0_attn_a_Wk1", "L0_attn_a_Wk2", "L0_attn_a_Wv", "L0_attn_a_Wc",
        "L0_attn_a_lq1", "L0_attn_a_lk1", "L0_attn_a_lq2", "L0_attn_a_lk2", "L0_attn_b_Wq", "L0_attn_b_Wk", "L0_attn_b_Wv",
        "L0_attn_b_Wo", "L0_attn_b_Wa", "L0_attn_b_ba", "L0_ffn_router_w", "L0_ffn_w_gate", "L0_ffn_w_up",
        "L0_ffn_w_down"]


def kernel(**inputs):
    import numpy as _np
    import concourse.bacc as _bacc
    from concourse.bass_utils import run_bass_kernel_spmd as _run

    nc = _bacc.Bacc("TRN2", target_bir_lowering=False, num_devices=1)
    arrays, io = {}, {}
    for name in _INS:
        a = _np.ascontiguousarray(inputs[name])
        arrays[f"in_{name}"] = a
        io[name] = nc.dram_tensor(f"in_{name}", a.shape, mybir.dt.from_np(a.dtype), kind="ExternalInput").ap()
    out = nc.dram_tensor("out_x", (2, 1024, 128), F32, kind="ExternalOutput").ap()
    program(nc, io, out)
    r = _run(nc, [arrays], core_ids=[0])
    return r.results[0]["out_x"]
```

```python
import math
from contextlib import ExitStack

import concourse.bass as bass
from concourse import mybir

F32 = mybir.dt.float32
BF16 = mybir.dt.bfloat16
U32 = mybir.dt.uint32
ALU = mybir.AluOpType
ACT = mybir.ActivationFunctionType
AX = mybir.AxisListType

P = 128
LAMBDA_INIT = 0.8 - 0.6 * math.exp(-0.3 * (2 - 1))
LN_EPS = 1e-5
NEG = -1e30
FIXED_COLUMNS = 128
MAXIMA_DONE = 0.87
TWO_BF16_ONES = 0x3F803F80


class Chain:

    def __init__(self, eng, sem, base=0):
        self.eng, self.sem, self.n, self.base = eng, sem, 0, base

    def link(self, ins):
        self.n += 1
        ins.then_inc(self.sem, 1)
        self.eng.wait_ge(self.sem, self.base + self.n)


def from_(t, lo):
    return not isinstance(t, int) or t >= lo


def over_pairs(eng, lo, hi, body, width=2):
    rounds = (hi - lo) // width
    with eng.Fori(0, rounds) as it:
        for k in range(width):
            body(it * width + (lo + k), (lo + k) % width)
    for s in range(lo + width * rounds, hi):
        body(s, s % width)


def layer_norm(nc, tag, X, XN, XNT, ident, NT, x_loaded=None, on_pool=None):
    with ExitStack() as ctx:
        stats = ctx.enter_context(nc.sbuf_tensor(f"{tag}_stats", [P, NT, 6], F32))
        mv = ctx.enter_context(nc.sbuf_tensor(f"{tag}_mv", [P, NT, 2], F32))
        ve = ctx.enter_context(nc.sbuf_tensor(f"{tag}_ve", [P, NT], F32))
        sd = ctx.enter_context(nc.sbuf_tensor(f"{tag}_sd", [P, NT], F32))
        rstd = ctx.enter_context(nc.sbuf_tensor(f"{tag}_rstd", [P, NT], F32))
        tp = ctx.enter_context(nc.psum_tensor(f"{tag}_tp", [P, 2, 512], F32))
        dve_step = nc.alloc_semaphore(f"{tag}_dve_step")
        var_ready = nc.alloc_semaphore(f"{tag}_var_ready")
        sd_ready = nc.alloc_semaphore(f"{tag}_sd_ready")
        xn_ready = nc.alloc_semaphore(f"{tag}_xn_ready")
        tp_ready = nc.alloc_semaphore(f"{tag}_tp_ready")
        tp_free = nc.alloc_semaphore(f"{tag}_tp_free")
        block = ctx.enter_context(nc.Block())

        if on_pool is not None:
            @block.gpsimd
            def _(pool):
                on_pool()

        @block.vector
        def _(dve):
            chain = Chain(dve, dve_step)
            for t in range(NT):
                if x_loaded is not None and t % 4 == 0:
                    dve.wait_ge(x_loaded[t // 4], 16)
                last = nc.vector.bn_stats(stats[:, t, :], X[:, t, :])
            chain.link(last)
            for t in range(NT):
                last = nc.vector.bn_aggr(mv[:, t, :], stats[:, t, :])
            chain.link(last)
            nc.vector.tensor_scalar_add(ve[:], mv[:, :, 1], LN_EPS).then_inc(var_ready, 1)
            dve.wait_ge(sd_ready, 1)
            chain.link(nc.vector.reciprocal(rstd[:], sd[:]))
            for t in range(NT):
                nc.vector.tensor_scalar(XN[:, t, :], X[:, t, :], mv[:, t, 0:1], rstd[:, t:t + 1],
                                        ALU.subtract, ALU.mult).then_inc(xn_ready, 1)

        @block.scalar
        def _(act):
            act.wait_ge(var_ready, 1)
            nc.scalar.activation(sd[:], ve[:], ACT.Sqrt).then_inc(sd_ready, 1)
            for q in range(NT // 4):
                act.wait_ge(tp_ready, q + 1)
                nc.scalar.activation(XNT[:, q * 512:(q + 1) * 512], tp[:, q % 2, :], ACT.Copy).then_inc(tp_free, 1)

        @block.tensor
        def _(pe):
            for t in range(NT):
                q = t // 4
                if t % 4 == 0 and q >= 2:
                    pe.wait_ge(tp_free, q - 1)
                pe.wait_ge(xn_ready, t + 1)
                last = nc.tensor.transpose(tp[:, q % 2, (t % 4) * P:(t % 4 + 1) * P], XN[:, t, :], ident[:])
                if t % 4 == 3:
                    last.then_inc(tp_ready, 1)


def diff_attention(nc, X, W3, ident, identb, io, scratch, load_next):
    NB, NTOK, D, H, HS = 2, 1024, 128, 16, 8
    NT = NB * NTOK // P
    KB = NTOK // P
    G = NB * H // 2
    U = 4
    VW = 32
    PARTS = ((0, 0), (0, 1), (0, 2), (1, 0), (1, 1), (2, 0))
    KR = 8 * len(PARTS)
    MR = P - 2
    KQ = P
    SC = 1.0 / math.sqrt(HS)
    QK = scratch["qk"]

    with ExitStack() as ctx:
        def sb(name, shape, dt=F32):
            return ctx.enter_context(nc.sbuf_tensor(name, shape, dt))

        def sem(name):
            return nc.alloc_semaphore(name)

        NQ = 3
        half = NQ * U * NTOK // 2
        VP = sb("VP", [P, G, KB, 2, VW])
        OT = sb("OT", [P, G, NTOK])
        lam = sb("lam", [P, H])

        with ExitStack() as c2:
            XNT = c2.enter_context(nc.sbuf_tensor("a_XNT", [P, NT * P], F32))
            W = c2.enter_context(nc.sbuf_tensor("a_W", [P, 4, P], F32))
            WP = c2.enter_context(nc.sbuf_tensor("a_WP", [P, 4, P], F32))
            w_turned = nc.alloc_semaphore("a_w_turned")
            WV = c2.enter_context(nc.sbuf_tensor("a_WV", [P, 2 * P], F32))
            LQ = c2.enter_context(nc.sbuf_tensor("a_LQ", [P, 4, H, HS], F32))
            lp = c2.enter_context(nc.sbuf_tensor("a_lp", [P, 2, H, HS], F32))
            ls = c2.enter_context(nc.sbuf_tensor("a_ls", [P, 2, H], F32))
            le = c2.enter_context(nc.sbuf_tensor("a_le", [P, 2, H], F32))
            w_loaded = nc.alloc_semaphore("a_w_loaded")
            x_loaded = [nc.alloc_semaphore(f"a_x_loaded{i}") for i in range(4)]
            NPT = 16
            parts = OT[:].rearrange("p g n -> p (g n)")[:, 0:NPT * 3 * 256].bitcast(BF16)\
                .rearrange("p (m a f) -> p m a f", m=NPT // 2, a=3)

            def part_of(n, part):
                return parts[:, n // 2, part, (n % 2) * 512:(n % 2 + 1) * 512]
            rest = c2.enter_context(nc.sbuf_tensor("a_rest", [P, 3, 512], F32))
            with ExitStack() as c3:
                XN = c3.enter_context(nc.sbuf_tensor("a_XN", [P, NT, D], F32))
                vpad = nc.alloc_semaphore("a_vpad")
                rows_set = nc.alloc_semaphore("a_rows_set")
                with nc.Block() as blk:
                    @blk.gpsimd
                    def _(pool):
                        nc.gpsimd.memset(VP[:], 0.0).then_inc(vpad, 1)
                        pool.wait_ge(vpad, 1)
                        nc.gpsimd.memset(VP[:, :, :, :, 16:17], 1.0).then_inc(vpad, 1)

                    @blk.vector
                    def _(dve):
                        nc.vector.memset(W3[:, 0:half].bitcast(U32), 0).then_inc(rows_set, 1)

                    @blk.sync
                    def _(sp):
                        xv = io["x"].rearrange("b (t p) d -> p (b t) d", p=P)
                        for c in range(4):
                            sp.dma_start(X[:, 4 * c:4 * c + 4, :], xv[:, 4 * c:4 * c + 4, :]).then_inc(x_loaded[c], 16)
                        for i, n in enumerate(("Wq1", "Wk1", "Wq2", "Wk2")):
                            sp.dma_start(W[:, i, :], io[n]).then_inc(w_loaded, 16)
                        sp.dma_start(WV[:], io["Wv"]).then_inc(w_loaded, 16)
                        for i, n in enumerate(("lq1", "lk1", "lq2", "lk2")):
                            sp.dma_start(LQ[:, i], io[n].partition_broadcast(P)).then_inc(w_loaded, 16)

                def keys_rows():
                    nc.gpsimd.memset(W3[0:96, half:2 * half].bitcast(U32), 0).then_inc(rows_set, 1)
                    nc.gpsimd.memset(W3[96:P, half:2 * half].bitcast(U32), TWO_BF16_ONES).then_inc(rows_set, 1)
                layer_norm(nc, "lna", X, XN, XNT, ident, NT, x_loaded, keys_rows)

            pp = c2.enter_context(nc.psum_tensor("a_pp", [P, 3, 512], F32))
            pv = c2.enter_context(nc.psum_tensor("a_pv", [P, 2, 512], F32))

            def s2(name):
                return nc.alloc_semaphore(name)

            qk_ready, qk_free, p0_ready, rest_ready, p1_ready, p2_ready = map(
                s2, ("a_qk_ready", "a_qk_free", "a_p0_ready", "a_rest_ready", "a_p1_ready", "a_p2_ready"))
            parts_stored = s2("a_parts_stored")
            v_ready, v_free, chain_s, lsum_ready, lexp_ready = map(
                s2, ("a_v_ready", "a_v_free", "a_chain", "a_lsum_ready", "a_lexp_ready"))
            items = [(att, qk, b, c) for b in range(NB) for att in range(2) for qk in range(2) for c in range(2)]
            with nc.Block() as block:
                @block.tensor
                def _(pe):
                    pe.wait_ge(w_loaded, 16 * 9)
                    pe.wait_ge(w_turned, 1)
                    for n, (att, qk, b, c) in enumerate(items):
                        if n >= 3:
                            pe.wait_ge(rest_ready, n - 2)
                        nc.tensor.matmul(pp[:, n % 3, :], WP[:, 2 * att + qk, :],
                                         XNT[:, b * NTOK + c * 512:b * NTOK + c * 512 + 512],
                                         start=True, stop=True).then_inc(qk_ready, 1)
                        t = n
                        if t >= 2:
                            pe.wait_ge(v_free, t - 1)
                        nc.tensor.matmul(pv[:, t % 2, 0:2 * P], XNT[:, t * P:(t + 1) * P], WV[:],
                                         start=True, stop=True).then_inc(v_ready, 1)

                @block.scalar
                def _(act):
                    act.wait_ge(lsum_ready, 1)
                    nc.scalar.activation(le[:], ls[:], ACT.Exp).then_inc(lexp_ready, 1)
                    for n in range(len(items) + 1):
                        if n < len(items):
                            act.wait_ge(qk_ready, n + 1)
                            nc.scalar.activation(part_of(n, 0), pp[:, n % 3, :], ACT.Copy).then_inc(p0_ready, 1)
                        if n:
                            act.wait_ge(rest_ready, n)
                            nc.scalar.activation(part_of(n - 1, 1), rest[:, (n - 1) % 3, :], ACT.Copy)\
                              .then_inc(p1_ready, 1)

                @block.vector
                def _(dve):
                    chain = Chain(dve, chain_s)
                    dve.wait_ge(w_loaded, 16 * 9)
                    nc.vector.tensor_copy(WP[:].rearrange("p i (d h) -> p i d h", h=H),
                                          W[:].rearrange("p i (h d) -> p i d h", h=H)).then_inc(w_turned, 1)
                    nc.vector.tensor_tensor(lp[:, 0], LQ[:, 0], LQ[:, 1], ALU.mult)
                    chain.link(nc.vector.tensor_tensor(lp[:, 1], LQ[:, 2], LQ[:, 3], ALU.mult))
                    nc.vector.reduce_sum(ls[:], lp[:], AX.X).then_inc(lsum_ready, 1)
                    dve.wait_ge(lexp_ready, 1)
                    chain.link(nc.vector.tensor_tensor(lam[:], le[:, 0], le[:, 1], ALU.subtract))
                    chain.link(nc.vector.tensor_scalar_add(lam[:], lam[:], LAMBDA_INIT))
                    for n in range(len(items)):
                        dve.wait_ge(p0_ready, n + 1)
                        if n >= 3:
                            dve.wait_ge(p2_ready, n - 2)
                        nc.vector.tensor_tensor(rest[:, n % 3, :], pp[:, n % 3, :], part_of(n, 0),
                                                ALU.subtract).then_inc(rest_ready, 1)
                        t = n
                        b, kb = divmod(t, KB)
                        dve.wait_ge(v_ready, t + 1)
                        if t == 0:
                            dve.wait_ge(vpad, 2)
                        nc.vector.tensor_copy(VP[:, b * 8:(b + 1) * 8, kb, :, 0:16],
                                              pv[:, t % 2, 0:2 * P].rearrange("p (g h v) -> p g h v", g=8, h=2))\
                          .then_inc(v_free, 1)

                @block.gpsimd
                def _(pool):
                    for n in range(len(items)):
                        pool.wait_ge(p1_ready, n + 1)
                        nc.gpsimd.tensor_tensor(part_of(n, 2), rest[:, n % 3, :], part_of(n, 1),
                                                ALU.subtract).then_inc(p2_ready, 1)

                @block.sync
                def _(sp):
                    for n, (att, qk, b, c) in enumerate(items):
                        if c == 0:
                            continue
                        sp.wait_ge(p2_ready, n + 1)
                        for part in range(3):
                            dst = QK[qk, part, :, b * 8:(b + 1) * 8, :, att, :]
                            sp.dma_start(dst.rearrange("d g h n -> d (g h) n"), parts[:, n // 2, part])\
                              .then_inc(parts_stored, 16)
                    sp.wait_ge(parts_stored, 16 * 3 * NPT // 2)

        with ExitStack() as c2:
            def s2(name):
                return nc.alloc_semaphore(name)

            QS, KS = (W3[:, i * half:(i + 1) * half].bitcast(BF16).rearrange("p (s u n) -> p s u n", s=NQ, u=U)
                      for i in range(2))
            VS = c2.enter_context(nc.sbuf_tensor("VS", [P, NQ, KB, 2, VW], F32))
            NPB = 8
            PB = c2.enter_context(nc.sbuf_tensor("PB", [P, NPB, 512], F32))
            maskb = c2.enter_context(nc.sbuf_tensor("maskb", [P, P], BF16))
            mx = c2.enter_context(nc.sbuf_tensor("mx", [P, 2, U, KB], F32))
            mxc = c2.enter_context(nc.sbuf_tensor("mxc", [P, U * KB], F32))
            mrow = c2.enter_context(nc.sbuf_tensor("mrow", [U * KB, 2, P], BF16))
            S1 = c2.enter_context(nc.psum_tensor("S1", [P, 3, 512], F32))
            S2 = c2.enter_context(nc.psum_tensor("S2", [P, 3, 512], F32))
            PV = c2.enter_context(nc.psum_tensor("PV", [P, 2, 512], F32))
            pool_init = s2("b_pool_init")
            const_s, g_loaded = s2("b_const"), [s2(f"g_loaded{i}") for i in range(NQ)]
            s1_done, s1_free, m_rows, mdve = map(
                s2, ("s1_done", "s1_free", "m_rows", "mdve"))
            s2_done, exp_done, mask_done, pv_done, pv_free, m_part = map(
                s2, ("s2_done", "exp_done", "mask_done", "pv_done", "pv_free", "m_part"))
            t1 = [(qb, c, u, min(512, (qb + 1) * P - c * 512)) for qb in range(KB)
                  for c in range(2) if (qb + 1) * P > c * 512 for u in range(U)]
            t2 = [(kb, c, u, max(kb * P, c * 512)) for kb, c in
                  ((0, 0), (0, 1), (1, 0), (1, 1), (4, 1), (3, 0), (2, 1), (5, 1), (2, 0), (7, 1), (6, 1), (3, 1))
                  for u in range(U)]
            last_of = [max(i for i, tile in enumerate(t2) if tile[1] == c) // U for c in range(2)]
            N1, N2 = len(t1) + 1, len(t2)
            ND = sum(1 for kb, c, u, q0 in t2 if q0 == kb * P and kb // 4 == c)
            NLOAD = 16 * (len(PARTS) + 3 + 1)
            diag_at = {}
            for i, (kb, c, u, q0) in enumerate(t2):
                if kb // 4 == c:
                    diag_at[i] = len(diag_at)
            assert len(t1) == N2 and N2 % NPB == 0 and N2 % 3 == 0 and len(diag_at) == ND and G % 3 == 1
            columns1 = [n + FIXED_COLUMNS for _, _, _, n in t1]
            columns2 = [(c + 1) * 512 - q0 for _, c, _, q0 in t2]
            max_upto = [0]
            for i in range(N2):
                share = (sum(columns2[:i]) + 512) / (MAXIMA_DONE * sum(columns2))
                m = max_upto[-1]
                while m < len(t1) and sum(columns1[:m + 1]) <= share * sum(columns1):
                    m += 1
                max_upto.append(m)
            assert max_upto[-2] == len(t1)
            gate = c2.enter_context(nc.sbuf_tensor("gate", [P, ND], F32))

            with nc.Block() as block:
                @block.sync
                def _(sp):
                    sp.wait_ge(const_s, 2)

                    def load(g, s):
                        for r, (part, _) in enumerate(PARTS):
                            src = QK[0, part, :, bass.ds(g, 1)].rearrange("d o h a n -> d (o h a n)")
                            sp.dma_start(QS[8 * r:8 * r + 8, s].rearrange("d u n -> d (u n)"),
                                         src).then_inc(g_loaded[s], 16)
                        for r, parts_here in ((0, 3), (3, 2), (5, 1)):
                            src = QK[1, 0:parts_here, :, bass.ds(g, 1)].rearrange("r d o h a n -> (r d) (o h a n)")
                            sp.dma_start(KS[8 * r:8 * (r + parts_here), s].rearrange("d u n -> d (u n)"), src)\
                              .then_inc(g_loaded[s], 16)
                        sp.dma_start(VS[:, s], VP[:, bass.ds(g, 1)].rearrange("p o k h v -> p (o k) h v"))\
                          .then_inc(g_loaded[s], 16)

                    def m_store(g, s):
                        sp.wait_ge(s1_free, (g + 1) * N1)
                        for t in range(2):
                            sp.dma_start(QS[MR + t:MR + t + 1, s].rearrange("t u (k q) -> t (u k) q", q=P),
                                         mrow[:, t]).then_inc(m_rows, 16)

                    load(0, 0)
                    load(1, 1)
                    m_store(0, 0)
                    with sp.Fori(0, (G - 4) // 3) as it:
                        for k in range(3):
                            g = it * 3 + k
                            sp.wait_ge(pv_free, g + 1)
                            load(g + 2, (k + 2) % 3)
                            m_store(g + 1, (k + 1) % 3)
                    for g in range(G - 4, G - 1):
                        if g + 2 < G:
                            sp.wait_ge(pv_free, g + 1)
                            load(g + 2, (g + 2) % 3)
                        m_store(g + 1, (g + 1) % 3)

                @block.tensor
                def _(pe):
                    pe.wait_ge(const_s, 2)

                    def max_tile(g, s, i, first=False):
                        if not (first and i < 3):
                            pe.wait_ge(s1_free, g * N1 + max(i - 2, 0))
                        qb, c, u, n = t1[i]
                        diag = n + c * 512 == (qb + 1) * P
                        ins = nc.tensor.matmul(S1[:, i % 3, 0:n], QS[0:MR, s, u, qb * P:(qb + 1) * P],
                                               KS[0:MR, s, u, c * 512:c * 512 + n], start=True, stop=not diag)
                        if diag:
                            ins = nc.tensor.matmul(S1[:, i % 3, n - P:n], identb[:], maskb[:], start=False, stop=True)
                        ins.then_inc(s1_done, 1)

                    def max_turn(g):
                        pe.wait_ge(m_part, g + 1)
                        nc.tensor.transpose(S1[0:U * KB, 0, 0:P], mxc[:], ident[:]).then_inc(s1_done, 1)

                    def score_tile(g, s, i):
                        kb, c, u, q0 = t2[i]
                        if i >= 3:
                            pe.wait_ge(exp_done, g * N2 + (i - 2))
                        nc.tensor.matmul(S2[:, i % 3, 0:(c + 1) * 512 - q0], KS[:, s, u, kb * P:(kb + 1) * P],
                                         QS[:, s, u, q0:(c + 1) * 512], start=True, stop=True).then_inc(s2_done, 1)

                    def value_tile(g, s, i):
                        kb, c, u, q0 = t2[i]
                        if i == 0:
                            pe.wait_ge(pv_free, g + 1)
                        pe.wait_ge(exp_done, g * N2 + (i + 1))
                        if i in diag_at:
                            pe.wait_ge(mask_done, g * ND + (diag_at[i] + 1))
                        nc.tensor.matmul(PV[32 * u:32 * u + 32, c, q0 - c * 512:512], VS[:, s, kb, u // 2, :],
                                         PB[:, i % NPB, 0:(c + 1) * 512 - q0], start=(kb == 0),
                                         stop=(i // U == last_of[c])).then_inc(pv_done, 1)

                    def step(g, s, next_loads):
                        pe.wait_ge(m_rows, (g + 1) * 32)
                        if next_loads is not None:
                            pe.wait_ge(g_loaded[(s + 1) % 3], next_loads * NLOAD)
                        for i in range(N2):
                            if next_loads is not None:
                                for m in range(max_upto[i], max_upto[i + 1]):
                                    max_tile(g + 1, (s + 1) % 3, m)
                                if max_upto[i] == N2 and max_upto[i - 1] < N2:
                                    max_turn(g + 1)
                            score_tile(g, s, i)
                            if i % U == 1 and i > U:
                                for j in range(i - U - 1, i - 1):
                                    value_tile(g, s, j)
                        for j in range(N2 - U, N2):
                            value_tile(g, s, j)

                    pe.wait_ge(g_loaded[0], NLOAD)
                    for i in range(N2):
                        max_tile(0, 0, i, first=True)
                    max_turn(0)
                    with pe.Fori(0, (G - 1) // 3) as it:
                        for k in range(3):
                            step(it * 3 + k, k, it + 1 if k < 2 else it + 2)
                    step(G - 1, (G - 1) % 3, None)

                @block.scalar
                def _(act):
                    with act.Fori(0, G) as g:
                        for i, (kb, c, u, q0) in enumerate(t2):
                            n = (c + 1) * 512 - q0
                            act.wait_ge(s2_done, g * N2 + (i + 1))
                            if i >= NPB:
                                act.wait_ge(pv_done, g * N2 + (i - NPB + 1))
                            nc.scalar.activation(PB[:, i % NPB, 0:n], S2[:, i % 3, 0:n], ACT.Exp, scale=SC)\
                              .then_inc(exp_done, 1)
                        act.wait_ge(pv_done, (g + 1) * N2)
                        nc.scalar.activation(OT[:, bass.ds(g, 1), :].rearrange("p o (c n) -> p (o c) n", c=2), PV[:], ACT.Copy)\
                          .then_inc(pv_free, 1)

                @block.gpsimd
                def _(pool):
                    nc.gpsimd.memset(maskb[:], 0.0).then_inc(pool_init, 1)
                    pool.wait_ge(pool_init, 1)
                    nc.gpsimd.affine_select(out=maskb[:], in_=maskb[:], compare_op=ALU.is_ge, fill=NEG, base=0,
                                            pattern=[[-1, P]], channel_multiplier=1).then_inc(const_s, 1)
                    with pool.Fori(0, G) as g:
                        for i in sorted(diag_at):
                            pool.wait_ge(exp_done, g * N2 + (i + 1))
                            nc.gpsimd.tensor_tensor(gate[:, diag_at[i]:diag_at[i] + 1], ident[:, 0:1], ident[:, 0:1], ALU.add)
                            nc.gpsimd.affine_select(out=PB[:, i % NPB, 0:P], in_=PB[:, i % NPB, 0:P],
                                                    compare_op=ALU.is_ge, fill=0.0, base=0, pattern=[[1, P]],
                                                    channel_multiplier=-1).then_inc(mask_done, 1)

                @block.vector
                def _(dve):
                    nc.vector.memset(mx[:], NEG).then_inc(const_s, 1)
                    nc.vector.memset(PV[:, 0, 0:1], 0.0).then_inc(pv_free, 1)
                    dve.wait_ge(const_s, 2)
                    with dve.Fori(0, G) as g:
                        for i, (qb, c, u, n) in enumerate(t1):
                            dve.wait_ge(s1_done, g * N1 + (i + 1))
                            last = nc.vector.reduce_max(mx[:, c, u, qb:qb + 1], S1[:, i % 3, 0:n], AX.X)
                            last.then_inc(s1_free, 1)
                        dve.wait_ge(s1_free, g * N1 + len(t1))
                        nc.vector.tensor_tensor(mxc[:], mx[:, 0].rearrange("p u k -> p (u k)"),
                                                mx[:, 1].rearrange("p u k -> p (u k)"), ALU.max).then_inc(m_part, 1)
                        dve.wait_ge(s1_done, (g + 1) * N1)
                        nc.vector.tensor_scalar(mrow[:, 0], S1[0:U * KB, 0, 0:P], -1.0, None, ALU.mult)\
                          .then_inc(mdve, 1)
                        dve.wait_ge(mdve, g + 1)
                        nc.vector.scalar_tensor_tensor(out=mrow[:, 1], in0=S1[0:U * KB, 0, 0:P], scalar=-1.0,
                                                       in1=mrow[:, 0], op0=ALU.mult, op1=ALU.subtract)\
                          .then_inc(s1_free, 1)


        with ExitStack() as c2:
            def sb2(name, shape, dt=F32):
                return c2.enter_context(nc.sbuf_tensor(name, shape, dt))

            def s2(name):
                return nc.alloc_semaphore(name)

            NP = NT // 2
            WC = sb2("WC", [P, 2, P])
            rd = sb2("rd", [P, 16, 2, 2])
            y1, y2, yc, sq, yn = (sb2(n, [P, 16, 2, 16]) for n in ("y1", "y2", "yc", "sq", "yn"))
            mean, var, sd, rs = (sb2(n, [P, 16, 2]) for n in ("mean", "var", "sd", "rs"))
            ynT = sb2("ynT", [P, 4, P])
            TP = c2.enter_context(nc.psum_tensor("TP", [P, 16, 2, 2, 32], F32))
            YT = c2.enter_context(nc.psum_tensor("YT", [P, 4, P], F32))
            OC = c2.enter_context(nc.psum_tensor("OC", [P, 512], F32))
            wc_loaded, tp_done, tp_free, c_step, var_ready, sd_ready, yn_ready, yt_done, ynt_ready, oc_done, x_added = map(
                s2, ("wc_loaded", "tp_done", "tp_free", "c_step", "c_var", "c_sd", "yn_ready", "yt_done", "ynt_ready",
                     "oc_done", "x_added"))
            with nc.Block() as block:
                @block.sync
                def _(sp):
                    sp.dma_start(WC[:], io["Wc"].rearrange("(k p) n -> p k n", p=P)).then_inc(wc_loaded, 16)
                    load_next(sp)

                @block.tensor
                def _(pe):
                    pe.wait_ge(wc_loaded, 16)
                    for pr in range(NP + 1):
                        if pr < NP:
                            if pr:
                                pe.wait_ge(tp_free, pr)
                            for t in range(2):
                                b, qb = divmod(2 * pr + t, KB)
                                for hp in range(8):
                                    last = nc.tensor.transpose(
                                        TP[:, 8 * t + hp].rearrange("p h a v -> p (h a v)"),
                                        OT[:, b * 8 + hp, qb * P:(qb + 1) * P], ident[:])
                            last.then_inc(tp_done, 1)
                        if pr:
                            pe.wait_ge(yn_ready, pr)
                            for j in range(4):
                                last = nc.tensor.transpose(YT[:, j], yn[:].rearrange("p k h v -> p (k h v)")[:, j * P:(j + 1) * P], ident[:])
                            last.then_inc(yt_done, 1)
                            pe.wait_ge(ynt_ready, pr)
                            if pr > 1:
                                pe.wait_ge(x_added, pr - 1)
                            for t in range(2):
                                for k in range(2):
                                    last = nc.tensor.matmul(OC[:, t * P:(t + 1) * P], ynT[:, 2 * t + k], WC[:, k],
                                                            start=(k == 0), stop=(k == 1))
                            last.then_inc(oc_done, 1)

                @block.scalar
                def _(act):
                    for pr in range(NP):
                        act.wait_ge(var_ready, pr + 1)
                        nc.scalar.activation(sd[:], var[:], ACT.Sqrt).then_inc(sd_ready, 1)
                        act.wait_ge(yt_done, pr + 1)
                        nc.scalar.activation(ynT[:], YT[:], ACT.Copy).then_inc(ynt_ready, 1)

                @block.vector
                def _(dve):
                    chain = Chain(dve, c_step)

                    def over_values(ap):
                        return ap.unsqueeze(3).to_broadcast([P, 16, 2, 16])

                    lam_b = lam[:].rearrange("p (k h) -> p k h", h=2).unsqueeze(1).to_broadcast([P, 2, 8, 2])

                    def add_out(pr):
                        dve.wait_ge(oc_done, pr + 1)
                        xs = X[:, 2 * pr:2 * pr + 2, :].rearrange("p t d -> p (t d)")
                        nc.vector.tensor_tensor(xs, xs, OC[:, 0:2 * P], ALU.add).then_inc(x_added, 1)

                    for pr in range(NP):
                        dve.wait_ge(tp_done, pr + 1)
                        chain.link(nc.vector.reciprocal(rd[:], TP[:, :, :, :, 16]))
                        r2 = rd[:, :, :, 1].rearrange("p (t k) h -> p t k h", t=2)
                        chain.link(nc.vector.tensor_tensor(r2, r2, lam_b, ALU.mult))
                        nc.vector.tensor_tensor(y1[:], TP[:, :, :, 0, 0:16], over_values(rd[:, :, :, 0]), ALU.mult)
                        ins = nc.vector.tensor_tensor(y2[:], TP[:, :, :, 1, 0:16], over_values(rd[:, :, :, 1]), ALU.mult)
                        ins.then_inc(tp_free, 1)
                        dve.wait_ge(tp_free, pr + 1)
                        chain.link(nc.vector.tensor_tensor(y1[:], y1[:], y2[:], ALU.subtract))
                        chain.link(nc.vector.reduce_sum(mean[:], y1[:], AX.X))
                        chain.link(nc.vector.tensor_scalar(mean[:], mean[:], 1.0 / 16, None, ALU.mult))
                        chain.link(nc.vector.tensor_tensor(yc[:], y1[:], over_values(mean[:]), ALU.subtract))
                        chain.link(nc.vector.tensor_tensor(sq[:], yc[:], yc[:], ALU.mult))
                        chain.link(nc.vector.reduce_sum(var[:], sq[:], AX.X))
                        nc.vector.tensor_scalar(var[:], var[:], 1.0 / 16, LN_EPS, ALU.mult, ALU.add).then_inc(var_ready, 1)
                        if pr:
                            add_out(pr - 1)
                        dve.wait_ge(sd_ready, pr + 1)
                        chain.link(nc.vector.reciprocal(rs[:], sd[:]))
                        chain.link(nc.vector.tensor_scalar(rs[:], rs[:], 1.0 - LAMBDA_INIT, None, ALU.mult))
                        dve.wait_ge(yt_done, pr)
                        nc.vector.tensor_tensor(yn[:], yc[:], over_values(rs[:]), ALU.mult).then_inc(yn_ready, 1)
                    add_out(NP - 1)


class Router:
    E, TOPK, FF = 8, 2, 512
    NT = 16
    SLOTS = NT * TOPK + E - 1


def load_experts(nc, sp, W3, io, loaded):
    E, FF = Router.E, Router.FF
    n = E * FF
    for i, name in enumerate(("w_gate", "w_up")):
        sp.dma_start(W3[:, i * n:(i + 1) * n].rearrange("p (e f) -> p e f", e=E),
                     io[name].rearrange("e p f -> p e f")).then_inc(loaded, 16)
    sp.dma_start(W3[:, 2 * n:3 * n].rearrange("p (e k d) -> p e k d", e=E, d=P),
                 io["w_down"].rearrange("e (k p) d -> p e k d", p=P)).then_inc(loaded, 16)


def moe(nc, tag, X, W3, ident, io, scratch, experts_loaded):
    E, FF, NT, SLOTS = Router.E, Router.FF, Router.NT, Router.SLOTS
    FK = FF // P
    NTOK, ROWS = NT * P, 2 * NT * P
    XD, YD = scratch["xn"], scratch["yd"]
    n = E * FF
    WG, WU = (W3[:, i * n:(i + 1) * n].rearrange("p (e f) -> p e f", e=E) for i in range(2))
    WD = W3[:, 2 * n:3 * n].rearrange("p (e k d) -> p e k d", e=E, d=P)

    with ExitStack() as ctx:
        def sb(name, shape, dt=F32):
            return ctx.enter_context(nc.sbuf_tensor(f"{tag}_{name}", shape, dt))

        def sem(name):
            return nc.alloc_semaphore(f"{tag}_{name}")

        wts = sb("wts", [P, 2, NT])
        source = sb("source", [P, SLOTS], U32)
        target = sb("target", [P, SLOTS], U32)
        etab = sb("etab", [1, SLOTS], U32)
        with ExitStack() as c2:
            def sb2(name, shape, dt=F32):
                return c2.enter_context(nc.sbuf_tensor(f"{tag}_{name}", shape, dt))

            def s2(name):
                return nc.alloc_semaphore(f"{tag}_{name}")

            XN = sb2("XN", [P, NT, P])
            XNT = sb2("XNT", [P, NT * P])
            layer_norm(nc, tag + "_ln", X, XN, XNT, ident, NT)

            RW = sb2("RW", [P, E])
            tri = sb2("tri", [P, P])
            ones = sb2("ones", [P, P])
            ioe = sb2("ioe", [P, E])
            iot = sb2("iot", [P, NT])
            ios = sb2("ios", [1, SLOTS])
            z, ex, prob, M, cnt, cinc, pos = (sb2(k, [P, NT, E]) for k in ("z", "ex", "prob", "M", "cnt", "cinc", "pos"))
            lmax, lsum, lrec, wsum, wrec = (sb2(k, [P, NT]) for k in ("lmax", "lsum", "lrec", "wsum", "wrec"))
            top = sb2("top", [P, NT, 8])
            tid = sb2("tid", [P, NT, 8], U32)
            tidf = sb2("tidf", [P, 2, NT])
            OH = sb2("OH", [P, 2, NT, E])
            sel = sb2("sel", [P, 2, NT, E])
            posf = sb2("posf", [P, 2, NT])
            over = sb2("over", [P, E, NT])
            tiles, ends, base = (sb2(k, [P, E]) for k in ("tiles", "ends", "base"))
            sover = sb2("sover", [1, SLOTS, E])
            sef = sb2("sef", [1, SLOTS])
            thr = sb2("thr", [P, SLOTS + 1])
            iol = sb2("iol", [P, P])
            iop = sb2("iop", [P, 1])
            spare = sb2("spare", [P, SLOTS])
            pair = sb2("pair", [P, 2 * NT])
            reached = sb2("reached", [P, 2 * NT, SLOTS + 1])
            slot_oh = sb2("slot_oh", [P, 2 * NT, SLOTS])
            place_oh = sb2("place_oh", [P, 2 * NT, P], BF16)
            marks = sb2("marks", [P, 2 * NT, 2, SLOTS], BF16)
            nreach, place = (sb2(k, [P, 2 * NT]) for k in ("nreach", "place"))
            A, B, second, empty, token = (sb2(k, [P, SLOTS]) for k in ("A", "B", "second", "empty", "token"))
            IV = c2.enter_context(nc.psum_tensor(f"{tag}_IV", [P, 512], F32))
            LG = c2.enter_context(nc.psum_tensor(f"{tag}_LG", [P, 512], F32))
            RC = c2.enter_context(nc.psum_tensor(f"{tag}_RC", [P, 4, NT, E], F32))
            rw_loaded, const_r, r_step, lg_done, z_ready, ex_ready, m_ready, rc_done, xn_stored, marked, placed, iv_done = map(
                s2, ("rw_loaded", "const_r", "r_step", "lg_done", "z_ready", "ex_ready", "m_ready", "rc_done", "xn_stored",
                     "marked", "placed", "iv_done"))
            with nc.Block() as block:
                @block.sync
                def _(sp):
                    with nc.allow_non_contiguous_dma("router weights, 4 KiB"):
                        sp.dma_start(RW[:], io["router_w"].rearrange("e d -> d e")).then_inc(rw_loaded, 16)
                    sp.dma_start(XD[:, :].rearrange("(t p) d -> p t d", p=P), XN[:]).then_inc(xn_stored, 16)
                    sp.wait_ge(xn_stored, 16)

                @block.gpsimd
                def _(pool):
                    nc.gpsimd.iota(ioe[:], [[1, E]], base=0, channel_multiplier=0,
                                   allow_small_or_imprecise_dtypes=True).then_inc(const_r, 1)
                    nc.gpsimd.iota(iot[:], [[P, NT]], base=0, channel_multiplier=0,
                                   allow_small_or_imprecise_dtypes=True).then_inc(const_r, 1)
                    nc.gpsimd.iota(ios[:], [[1, SLOTS]], base=0, channel_multiplier=0,
                                   allow_small_or_imprecise_dtypes=True).then_inc(const_r, 1)
                    nc.gpsimd.iota(thr[:], [[P, SLOTS + 1]], base=0, channel_multiplier=0,
                                   allow_small_or_imprecise_dtypes=True).then_inc(const_r, 1)
                    nc.gpsimd.iota(iol[:], [[1, P]], base=-P, channel_multiplier=0,
                                   allow_small_or_imprecise_dtypes=True).then_inc(const_r, 1)
                    nc.gpsimd.iota(iop[:], [[0, 1]], base=0, channel_multiplier=1,
                                   allow_small_or_imprecise_dtypes=True).then_inc(const_r, 1)
                    nc.gpsimd.iota(spare[:], [[P, SLOTS]], base=ROWS + P, channel_multiplier=1,
                                   allow_small_or_imprecise_dtypes=True).then_inc(const_r, 1)
                    nc.gpsimd.iota(pair[:], [[1, 2 * NT]], base=1, channel_multiplier=0,
                                   allow_small_or_imprecise_dtypes=True).then_inc(const_r, 1)
                    nc.gpsimd.memset(ones[:], 1.0).then_inc(const_r, 1)
                    nc.gpsimd.memset(tri[:], 1.0).then_inc(const_r, 1)
                    pool.wait_ge(const_r, 10)
                    nc.gpsimd.affine_select(out=tri[:], in_=tri[:], compare_op=ALU.is_gt, fill=0.0, base=0,
                                            pattern=[[1, P]], channel_multiplier=-1).then_inc(const_r, 1)
                @block.tensor
                def _(pe):
                    pe.wait_ge(rw_loaded, 16)
                    for t in range(NT):
                        last = nc.tensor.matmul(LG[:, t * E:(t + 1) * E], XNT[:, t * P:(t + 1) * P], RW[:],
                                                start=True, stop=True)
                    last.then_inc(lg_done, 1)
                    pe.wait_ge(const_r, 11)
                    pe.wait_ge(m_ready, 1)
                    Mf = M[:].rearrange("p t e -> p (t e)")
                    nc.tensor.matmul(RC[:, 0].rearrange("p t e -> p (t e)"), tri[:], Mf, start=True, stop=True)
                    nc.tensor.matmul(RC[:, 1].rearrange("p t e -> p (t e)"), ones[:], Mf, start=True, stop=True)\
                      .then_inc(rc_done, 1)
                    pe.wait_ge(marked, 1)
                    for i in range(2 * NT):
                        if i % 8 == 0:
                            pe.wait_ge(placed, i // 8 + 1)
                        last = nc.tensor.matmul(IV[:, 0:2 * SLOTS], place_oh[:, i], marks[:, i].rearrange("p a s -> p (a s)"),
                                                start=(i == 0), stop=(i == 2 * NT - 1))
                    last.then_inc(iv_done, 1)

                @block.scalar
                def _(act):
                    act.wait_ge(z_ready, 1)
                    nc.scalar.activation(ex[:], z[:], ACT.Exp).then_inc(ex_ready, 1)

                @block.vector
                def _(dve):
                    chain = Chain(dve, r_step)

                    def per_tile(ap):
                        return ap.unsqueeze(2).to_broadcast([P, NT, E])

                    lg = LG[:, 0:NT * E].rearrange("p (t e) -> p t e", e=E)
                    dve.wait_ge(lg_done, 1)
                    chain.link(nc.vector.reduce_max(lmax[:], lg, AX.X))
                    nc.vector.tensor_tensor(z[:], lg, per_tile(lmax[:]), ALU.subtract).then_inc(z_ready, 1)
                    dve.wait_ge(ex_ready, 1)
                    chain.link(nc.vector.reduce_sum(lsum[:], ex[:], AX.X))
                    chain.link(nc.vector.reciprocal(lrec[:], lsum[:]))
                    chain.link(nc.vector.tensor_tensor(prob[:], ex[:], per_tile(lrec[:]), ALU.mult))
                    for t in range(NT):
                        last = nc.vector.max(top[:, t, :], prob[:, t, :])
                    chain.link(last)
                    for t in range(NT):
                        last = nc.vector.max_index(tid[:, t, :], top[:, t, :], prob[:, t, :])
                    nc.vector.tensor_tensor(wsum[:], top[:, :, 0], top[:, :, 1], ALU.add)
                    chain.link(last)
                    chain.link(nc.vector.tensor_copy(tidf[:], tid[:, :, 0:2].rearrange("p t k -> p k t")))
                    chain.link(nc.vector.reciprocal(wrec[:], wsum[:]))
                    for k in range(2):
                        nc.vector.tensor_tensor(wts[:, k], top[:, :, k], wrec[:], ALU.mult)
                    dve.wait_ge(const_r, 11)
                    for k in range(2):
                        last = nc.vector.tensor_tensor(OH[:, k], ioe[:].unsqueeze(1).to_broadcast([P, NT, E]),
                                                       per_tile(tidf[:, k]), ALU.is_equal)
                    chain.link(last)
                    nc.vector.tensor_tensor(M[:], OH[:, 0], OH[:, 1], ALU.add).then_inc(m_ready, 1)
                    dve.wait_ge(rc_done, 1)
                    chain.link(nc.vector.tensor_copy(cnt[:], RC[:, 1]))
                    for e in range(E):
                        last = nc.vector.tensor_tensor_scan(out=cinc[:, :, e], data0=ones[:, 0:NT], data1=cnt[:, :, e],
                                                            initial=0.0, op0=ALU.mult, op1=ALU.add)
                    chain.link(last)
                    chain.link(nc.vector.tensor_tensor(over[:], cinc[:, NT - 1, :].unsqueeze(2).to_broadcast([P, E, NT]),
                                                       iot[:].unsqueeze(1).to_broadcast([P, E, NT]), ALU.is_gt))
                    chain.link(nc.vector.reduce_sum(tiles[:], over[:], AX.X))
                    chain.link(nc.vector.tensor_tensor_scan(out=ends[:], data0=ones[:, 0:E], data1=tiles[:], initial=0.0,
                                                            op0=ALU.mult, op1=ALU.add))
                    chain.link(nc.vector.tensor_tensor(base[:], ends[:], tiles[:], ALU.subtract))
                    chain.link(nc.vector.tensor_scalar(base[:], base[:], float(P), None, ALU.mult))
                    chain.link(nc.vector.tensor_tensor(pos[:], cinc[:], cnt[:], ALU.subtract))
                    chain.link(nc.vector.tensor_tensor(pos[:], pos[:], RC[:, 0], ALU.add))
                    chain.link(nc.vector.tensor_tensor(pos[:], pos[:], base[:].unsqueeze(1).to_broadcast([P, NT, E]), ALU.add))
                    for k in range(2):
                        last = nc.vector.tensor_tensor(sel[:, k], pos[:], OH[:, k], ALU.mult)
                    chain.link(last)
                    chain.link(nc.vector.reduce_sum(posf[:], sel[:], AX.X))
                    pf = posf[:].rearrange("p k t -> p (k t)")
                    chain.link(nc.vector.tensor_tensor(reached[:], pf.unsqueeze(2).to_broadcast([P, 2 * NT, SLOTS + 1]),
                                                       thr[:].unsqueeze(1).to_broadcast([P, 2 * NT, SLOTS + 1]), ALU.is_ge))
                    chain.link(nc.vector.reduce_sum(nreach[:], reached[:], AX.X))
                    chain.link(nc.vector.scalar_tensor_tensor(out=place[:], in0=nreach[:], scalar=-float(P), in1=pf,
                                                              op0=ALU.mult, op1=ALU.add))
                    chain.link(nc.vector.tensor_tensor(slot_oh[:], reached[:, :, 0:SLOTS], reached[:, :, 1:SLOTS + 1],
                                                       ALU.subtract))
                    nc.vector.tensor_tensor(marks[:, :, 0], slot_oh[:], pair[:].unsqueeze(2)
                                            .to_broadcast([P, 2 * NT, SLOTS]), ALU.mult)
                    nc.vector.tensor_scalar(marks[:, :, 1], slot_oh[:], iop[:, 0:1], None, ALU.mult).then_inc(marked, 1)
                    for q in range(4):
                        i = slice(8 * q, 8 * q + 8)
                        nc.vector.tensor_tensor(place_oh[:, i], iol[:].unsqueeze(1).to_broadcast([P, 8, P]),
                                                place[:, i].unsqueeze(2).to_broadcast([P, 8, P]), ALU.is_equal)\
                          .then_inc(placed, 1)
                    chain.link(nc.vector.tensor_tensor(sover[:], ios[:].unsqueeze(2).to_broadcast([1, SLOTS, E]),
                                                       ends[0:1, :].unsqueeze(1).to_broadcast([1, SLOTS, E]), ALU.is_ge))
                    chain.link(nc.vector.reduce_sum(sef[:], sover[:], AX.X))
                    nc.vector.tensor_scalar(etab[:], sef[:], float(E - 1), None, ALU.min)
                    dve.wait_ge(iv_done, 1)
                    nc.vector.tensor_copy(A[:], IV[:, 0:SLOTS])
                    chain.link(nc.vector.tensor_scalar_add(B[:], IV[:, SLOTS:2 * SLOTS], -float(P)))
                    nc.vector.tensor_scalar(second[:], A[:], float(NT + 1), -float(NT), ALU.is_ge, ALU.mult)
                    chain.link(nc.vector.scalar_tensor_tensor(out=empty[:], in0=A[:], scalar=0.0, in1=spare[:], op0=ALU.is_equal,
                                                              op1=ALU.mult))
                    chain.link(nc.vector.tensor_tensor(second[:], second[:], A[:], ALU.add))
                    nc.vector.scalar_tensor_tensor(out=token[:], in0=second[:], scalar=float(P), in1=B[:], op0=ALU.mult,
                                                   op1=ALU.add)
                    chain.link(nc.vector.scalar_tensor_tensor(out=B[:], in0=A[:], scalar=float(P), in1=B[:], op0=ALU.mult,
                                                              op1=ALU.add))
                    nc.vector.tensor_scalar(source[:], token[:], 0.0, None, ALU.max)
                    nc.vector.tensor_tensor(target[:], B[:], empty[:], ALU.add)

        XB = 4
        with ExitStack() as c2:
            def sb2(name, shape, dt=F32):
                return c2.enter_context(nc.sbuf_tensor(f"{tag}_{name}", shape, dt))

            def s2(name):
                return nc.alloc_semaphore(f"{tag}_{name}")

            xs = sb2("xs", [P, XB, P])
            xt = sb2("xt", [P, 2, P])
            gs = sb2("gs", [P, 2, FF])
            hs = sb2("hs", [P, 2, FF])
            ht = sb2("ht", [P, 2, FF])
            ys = sb2("ys", [P, 2, P])
            XT = c2.enter_context(nc.psum_tensor(f"{tag}_XT", [P, 512], F32))
            GP = c2.enter_context(nc.psum_tensor(f"{tag}_GP", [P, 2, FF], F32))
            UP = c2.enter_context(nc.psum_tensor(f"{tag}_UP", [P, 2, FF], F32))
            HT = c2.enter_context(nc.psum_tensor(f"{tag}_HT", [P, FF], F32))
            YP = c2.enter_context(nc.psum_tensor(f"{tag}_YP", [P, 512], F32))
            xs_loaded = [s2(f"xs_loaded{i}") for i in range(XB)]
            ys_stored = [s2(f"ys_stored{i}") for i in range(2)]
            xt_done, xt_copied, g_done, u_done, silu_done, h_ready, ht_done, ht_copied, y_done, y_copied = map(
                s2, ("xt_done", "xt_copied", "g_done", "u_done", "silu_done", "h_ready", "ht_done", "ht_copied", "y_done",
                     "y_copied"))

            with nc.Block() as block:
                @block.gpsimd
                def _(pool):
                    def gather(s):
                        if s >= XB:
                            pool.wait_ge(xt_done, s - XB + 1)
                        pool.indirect_dma_start(out=xs[:, s % XB], out_offset=None, in_=XD[:, :],
                                                in_offset=bass.IndirectOffsetOnAxis(ap=source[:, s:s + 1], axis=0))\
                            .then_inc(xs_loaded[s % XB], 16)

                    def scatter(s):
                        pool.wait_ge(y_copied, s + 1)
                        pool.indirect_dma_start(out=YD[:, :], out_offset=bass.IndirectOffsetOnAxis(
                            ap=target[:, s:s + 1], axis=0), in_=ys[:, s % 2], in_offset=None)\
                            .then_inc(ys_stored[s % 2], 16)

                    for s in range(XB):
                        gather(s)
                    for s in range(SLOTS):
                        if s + XB < SLOTS:
                            gather(s + XB)
                        scatter(s)
                    pool.wait_ge(ys_stored[0], 16 * ((SLOTS + 1) // 2))
                    pool.wait_ge(ys_stored[1], 16 * (SLOTS // 2))

                @block.tensor
                def _(pe):
                    def x_turn(s, b):
                        pe.wait_ge(xs_loaded[b], (s - b) // XB * 16 + 16 if isinstance(s, int) else (s - b) * (16 // XB) + 16)
                        if from_(s, 1):
                            pe.wait_ge(xt_copied, s)
                        nc.tensor.transpose(XT[:, 0:P], xs[:, b], ident[:]).then_inc(xt_done, 1)

                    def expert(s):
                        return pe.value_load(etab[0:1, bass.ds(s, 1)], min_val=0, max_val=E - 1)

                    def up(s, b):
                        e = expert(s)
                        pe.wait_ge(xt_copied, s + 1)
                        nc.tensor.matmul(GP[:, b], xt[:, b], WG[:, bass.ds(e, 1), :].rearrange("p o f -> p (o f)"),
                                         start=True, stop=True).then_inc(g_done, 1)
                        nc.tensor.matmul(UP[:, b], xt[:, b], WU[:, bass.ds(e, 1), :].rearrange("p o f -> p (o f)"),
                                         start=True, stop=True).then_inc(u_done, 1)

                    def h_turn(s, b):
                        pe.wait_ge(h_ready, s + 1)
                        if from_(s, 1):
                            pe.wait_ge(ht_copied, s)
                        for j in range(FK):
                            last = nc.tensor.transpose(HT[:, j * P:(j + 1) * P], hs[:, b, j * P:(j + 1) * P], ident[:])
                        last.then_inc(ht_done, 1)

                    def down(s, b):
                        e = expert(s)
                        pe.wait_ge(ht_copied, s + 1)
                        if from_(s, 1):
                            pe.wait_ge(y_copied, s)
                        for j in range(FK):
                            last = nc.tensor.matmul(YP[:, 0:P], ht[:, b, j * P:(j + 1) * P],
                                                    WD[:, bass.ds(e, 1), j, :].rearrange("p o d -> p (o d)"),
                                                    start=(j == 0), stop=(j == FK - 1))
                        last.then_inc(y_done, 1)

                    def step(s, b):
                        up(s + 1, (b + 1) % 2)
                        h_turn(s, b % 2)
                        x_turn(s + 2, (b + 2) % XB)
                        down(s - 1, (b + 1) % 2)

                    pe.wait_ge(experts_loaded, 48)
                    x_turn(0, 0)
                    up(0, 0)
                    x_turn(1, 1)
                    up(1, 1)
                    h_turn(0, 0)
                    x_turn(2, 2)
                    over_pairs(pe, 1, SLOTS - 2, step, XB)
                    s = SLOTS - 2
                    up(s + 1, (s + 1) % 2)
                    h_turn(s, s % 2)
                    down(s - 1, (s - 1) % 2)
                    h_turn(s + 1, (s + 1) % 2)
                    down(s, s % 2)
                    down(s + 1, (s + 1) % 2)

                @block.scalar
                def _(act):
                    def x_copy(s, b):
                        act.wait_ge(xt_done, s + 1)
                        nc.scalar.activation(xt[:, b], XT[:, 0:P], ACT.Copy).then_inc(xt_copied, 1)

                    def silu(s, b):
                        act.wait_ge(g_done, s + 1)
                        nc.scalar.activation(gs[:, b], GP[:, b], ACT.Silu).then_inc(silu_done, 1)

                    def h_copy(s, b):
                        act.wait_ge(ht_done, s + 1)
                        nc.scalar.activation(ht[:, b], HT[:], ACT.Copy).then_inc(ht_copied, 1)

                    def body(s, b):
                        silu(s, b)
                        h_copy(s - 1, 1 - b)
                        x_copy(s + 1, 1 - b)
                    x_copy(0, 0)
                    silu(0, 0)
                    x_copy(1, 1)
                    over_pairs(act, 1, SLOTS - 1, body)
                    s = SLOTS - 1
                    silu(s, s % 2)
                    h_copy(s - 1, (s - 1) % 2)
                    h_copy(s, s % 2)

                @block.vector
                def _(dve):
                    def gate(s, b):
                        dve.wait_ge(silu_done, s + 1)
                        dve.wait_ge(u_done, s + 1)
                        nc.vector.tensor_tensor(hs[:, b], gs[:, b], UP[:, b], ALU.mult).then_inc(h_ready, 1)

                    def y_copy(s, b):
                        dve.wait_ge(y_done, s + 1)
                        if not isinstance(s, int) or s >= 2:
                            dve.wait_ge(ys_stored[b], (s - b) * 8)
                        nc.vector.tensor_copy(ys[:, b], YP[:, 0:P]).then_inc(y_copied, 1)

                    def body(s, b):
                        gate(s, b)
                        y_copy(s - 2, b)
                    gate(0, 0)
                    gate(1, 1)
                    body(2, 0)
                    body(3, 1)
                    over_pairs(dve, 4, SLOTS, body)
                    y_copy(SLOTS - 2, SLOTS % 2)
                    y_copy(SLOTS - 1, (SLOTS - 1) % 2)

        with ExitStack() as c2:
            GB = c2.enter_context(nc.sbuf_tensor(f"{tag}_GB", [P, NT, 2, P], F32))
            gathered = [nc.alloc_semaphore(f"{tag}_gathered{i}") for i in range(4)]
            added = nc.alloc_semaphore(f"{tag}_added")
            with nc.Block() as block:
                @block.sync
                def _(sp):
                    for q in range(4):
                        for k in range(2):
                            rows = slice(k * NTOK + q * 4 * P, k * NTOK + (q + 1) * 4 * P)
                            sp.dma_start(GB[:, 4 * q:4 * q + 4, k], YD[rows, :].rearrange("(t p) d -> p t d", p=P))\
                              .then_inc(gathered[q], 16)

                @block.vector
                def _(dve):
                    for q in range(4):
                        dve.wait_ge(gathered[q], 16 * 2)
                        for k in range(2):
                            if k:
                                dve.wait_ge(added, 4 * (2 * q + 1))
                            for t in range(4 * q, 4 * q + 4):
                                nc.vector.scalar_tensor_tensor(out=X[:, t, :], in0=GB[:, t, k, :], scalar=wts[:, k, t:t + 1],
                                                               in1=X[:, t, :], op0=ALU.mult, op1=ALU.add).then_inc(added, 1)


def decay_attention(nc, X, ident, identb, io):
    NT, CPS, D, H, DH = 16, 8, 128, 16, 64
    HP, HG = H // 2, 4
    VW = DH + 1
    EPS, SHIFT = 1e-6, 2.0

    with ExitStack() as ctx:
        def sb(name, shape, dt=F32):
            return ctx.enter_context(nc.sbuf_tensor("d_" + name, shape, dt))

        def sem(name):
            return nc.alloc_semaphore("d_" + name)

        XNT = sb("XNT", [P, NT * P])
        WQ, WK, WV = (sb(n, [P, H * DH]) for n in ("WQ", "WK", "WV"))
        WO = sb("WO", [P, HP, D])
        WA = sb("WA", [P, H])
        ba = sb("ba", [P, H])
        triu = sb("triu", [P, P])
        later = sb("later", [P, P], BF16)
        LT = sb("LT", [3 * H, NT, P], BF16)
        pick = sb("pick", [3 * H, H, P], BF16)
        ones = sb("ones", [P, P])
        la, L, nL, eL, wk, rem = (sb(n, [P, NT, H]) for n in ("la", "L", "nL", "eL", "wk", "rem"))
        dec = sb("dec", [P, NT, HP])
        S = sb("S", [P, HP, 2, VW])
        V1 = sb("V1", [P, 2, H, VW])
        wb_loaded = sem("w_loaded")
        with ExitStack() as c2:
            XN = c2.enter_context(nc.sbuf_tensor("d_XN", [P, NT, P], F32))
            with nc.Block() as blk:
                @blk.sync
                def _(sp):
                    for w, n in ((WA, "Wa"), (WK, "Wk"), (WV, "Wv"), (WQ, "Wq")):
                        sp.dma_start(w[:], io[n]).then_inc(wb_loaded, 16)
                    sp.dma_start(ba[:], io["ba"].partition_broadcast(P)).then_inc(wb_loaded, 16)
                    sp.dma_start(WO[:], io["Wo"].rearrange("(k p) d -> p k d", p=P)).then_inc(wb_loaded, 16)
            layer_norm(nc, "d_ln", X, XN, XNT, ident, NT)

        with ExitStack() as c2:
            zz, mz, ez, lz = (c2.enter_context(nc.sbuf_tensor("d_" + n, [P, NT, H], F32)) for n in ("zz", "mz", "ez", "lz"))
            ZP = c2.enter_context(nc.psum_tensor("d_ZP", [P, 512], F32))
            LP = c2.enter_context(nc.psum_tensor("d_LP", [P, 512], F32))
            TP = c2.enter_context(nc.psum_tensor("d_TP", [P, 512], F32))
            LTP = c2.enter_context(nc.psum_tensor("d_LTP", [3 * H, NT // 4, 512], F32))
            Lp = c2.enter_context(nc.sbuf_tensor("d_Lp", [P, NT, 3, H], BF16))
            Lr = c2.enter_context(nc.sbuf_tensor("d_Lr", [P, NT, H], F32))
            const_d, z_done, step, mz_ready, ez_ready, ez1_ready, lz_ready, la_ready, l_done, rem_ready, l_ready, e_ready, lp_ready, lt_done = map(
                lambda n: nc.alloc_semaphore("d_" + n),
                ("const", "z_done", "step", "mz_ready", "ez_ready", "ez1_ready", "lz_ready", "la_ready", "l_done",
                 "rem_ready", "l_ready", "e_ready", "lp_ready", "lt_done"))
            with nc.Block() as block:
                @block.gpsimd
                def _(pool):
                    nc.gpsimd.memset(ones[:], 1.0).then_inc(const_d, 1)
                    nc.gpsimd.memset(triu[:], 1.0).then_inc(const_d, 1)
                    pool.wait_ge(const_d, 2)
                    nc.gpsimd.affine_select(out=triu[:], in_=triu[:], compare_op=ALU.is_ge, fill=0.0, base=0,
                                            pattern=[[1, P]], channel_multiplier=-1).then_inc(const_d, 1)
                    nc.gpsimd.memset(later[:], 0.0).then_inc(const_d, 1)
                    pool.wait_ge(const_d, 4)
                    nc.gpsimd.affine_select(out=later[:], in_=later[:], compare_op=ALU.is_ge, fill=NEG, base=0,
                                            pattern=[[1, P]], channel_multiplier=-1).then_inc(const_d, 1)
                    nc.gpsimd.memset(S[:], 0.0).then_inc(const_d, 1)
                    nc.gpsimd.memset(V1[:], 1.0).then_inc(const_d, 1)
                    nc.gpsimd.memset(pick[:], 0.0).then_inc(const_d, 1)
                    for part in range(3):
                        pool.wait_ge(const_d, 8 + part)
                        nc.gpsimd.affine_select(out=pick[:], in_=pick[:], compare_op=ALU.not_equal, fill=1.0,
                                                base=-H * part, pattern=[[-1, H], [0, P]],
                                                channel_multiplier=1).then_inc(const_d, 1)

                @block.tensor
                def _(pe):
                    pe.wait_ge(wb_loaded, 16 * 6)
                    for t in range(NT):
                        last = nc.tensor.matmul(ZP[:, t * H:(t + 1) * H], XNT[:, t * P:(t + 1) * P], WA[:],
                                                start=True, stop=True)
                    last.then_inc(z_done, 1)
                    pe.wait_ge(const_d, 7)
                    pe.wait_ge(la_ready, 1)
                    laf = la[:].rearrange("p t h -> p (t h)")
                    nc.tensor.matmul(LP[:, 0:NT * H], triu[:], laf, start=True, stop=True)
                    nc.tensor.matmul(TP[:, 0:NT * H], ones[:], laf, start=True, stop=True).then_inc(l_done, 1)
                    pe.wait_ge(lp_ready, 1)
                    for t in range(NT):
                        nc.tensor.matmul(LTP[:, t // 4, (t % 4) * P:(t % 4 + 1) * P],
                                         Lp[:, t].rearrange("p a h -> p (a h)"), identb[:],
                                         start=True, stop=True).then_inc(lt_done, 1)

                @block.scalar
                def _(act):
                    act.wait_ge(mz_ready, 1)
                    nc.scalar.activation(ez[:], mz[:], ACT.Exp).then_inc(ez_ready, 1)
                    act.wait_ge(ez1_ready, 1)
                    nc.scalar.activation(lz[:], ez[:], ACT.Ln).then_inc(lz_ready, 1)
                    act.wait_ge(l_ready, 1)
                    nc.scalar.activation(eL[:], L[:], ACT.Exp).then_inc(e_ready, 1)
                    act.wait_ge(rem_ready, 1)
                    nc.scalar.activation(wk[:], rem[:], ACT.Exp).then_inc(e_ready, 1)
                    tp = TP[:, 0:NT * H].rearrange("p (t k h) -> p t k h", t=NT, h=2)
                    for h in range(2):
                        q = slice(64 * h, 64 * h + 64)
                        nc.scalar.activation(dec[q], tp[q, :, :, h], ACT.Exp).then_inc(e_ready, 1)
                    for q in range(NT // 4):
                        act.wait_ge(lt_done, 4 * q + 4)
                        nc.scalar.activation(LT[:, 4 * q:4 * q + 4].rearrange("p t n -> p (t n)"), LTP[:, q], ACT.Copy)

                @block.vector
                def _(dve):
                    chain = Chain(dve, step)
                    dve.wait_ge(z_done, 1)
                    zp = ZP[:, 0:NT * H].rearrange("p (t h) -> p t h", h=H)
                    chain.link(nc.vector.tensor_tensor(zz[:], zp, ba[:].unsqueeze(1).to_broadcast([P, NT, H]), ALU.add))
                    chain.link(nc.vector.tensor_scalar_add(zz[:], zz[:], SHIFT))
                    nc.vector.scalar_tensor_tensor(out=mz[:], in0=zz[:], scalar=-1.0, in1=zz[:], op0=ALU.mult,
                                                   op1=ALU.min).then_inc(mz_ready, 1)
                    dve.wait_ge(ez_ready, 1)
                    nc.vector.tensor_scalar_add(ez[:], ez[:], 1.0).then_inc(ez1_ready, 1)
                    dve.wait_ge(lz_ready, 1)
                    nc.vector.scalar_tensor_tensor(out=la[:], in0=zz[:], scalar=0.0, in1=lz[:], op0=ALU.min,
                                                   op1=ALU.subtract).then_inc(la_ready, 1)
                    dve.wait_ge(l_done, 1)
                    nc.vector.tensor_copy(L[:].rearrange("p t h -> p (t h)"), LP[:, 0:NT * H]).then_inc(l_ready, 1)
                    dve.wait_ge(l_ready, 1)
                    nc.vector.tensor_tensor(rem[:].rearrange("p t h -> p (t h)"), TP[:, 0:NT * H],
                                            L[:].rearrange("p t h -> p (t h)"), ALU.subtract).then_inc(rem_ready, 1)
                    nc.vector.tensor_scalar_mul(nL[:], L[:], -1.0)
                    chain.link(nc.vector.tensor_copy(Lp[:, :, 0], L[:]))
                    chain.link(nc.vector.tensor_tensor(Lr[:], L[:], Lp[:, :, 0], ALU.subtract))
                    chain.link(nc.vector.tensor_copy(Lp[:, :, 1], Lr[:]))
                    nc.vector.tensor_tensor(Lp[:, :, 2], Lr[:], Lp[:, :, 1], ALU.subtract).then_inc(lp_ready, 1)
                    dve.wait_ge(e_ready, 4)
                    for t in range(0, NT, CPS):
                        nc.vector.memset(eL[:, t, :], 0.0)
                        nc.vector.memset(dec[:, t, :], 0.0)

        xc = sb("xc", [P, 2, P])
        nlc = sb("nlc", [P, 2, H])
        etmp = sb("etmp", [P, 4, 512])
        enegs = sb("enegs", [P, 4, 512])
        Kn = sb("Kn", [P, 2, H * DH])
        QT = sb("QT", [P, 2, HP, P])
        KTZ = sb("KTZ", [P, 2, HP, 2, P])
        KS = sb("KS", [P, 2, H * DH])
        SD = sb("SD", [P, HP, 2, VW])
        DM = sb("DM", [P, 2, 4, P])
        WB = sb("WB", [P, 2, 4, P])
        ox = sb("ox", [P, 4, VW])
        O = sb("O", [P, 2, H, VW])
        rd = sb("rd", [P, H])
        YN = sb("YN", [P, H * DH])
        YTS = sb("YTS", [P, HP, P])

        def psum(name, shape):
            return ctx.enter_context(nc.psum_tensor("d_" + name, shape, F32))

        PA, AT, LB = psum("PA", [P, 2, 512]), psum("AT", [P, 4, P]), psum("LB", [P, 4, P])
        OI, OX = psum("OI", [P, 512]), psum("OX", [P, 512])
        TR, SU = psum("TR", [P, 4, P]), psum("SU", [P, 512])
        names = ("ktz_zero", "xc_ready", "proj_done", "elu_done", "v_done", "exp_done", "yt_done", "yt_copied", "kt_done",
                 "kt_copied", "lb_done", "at_done", "expd_done", "neg_done", "w_done", "inter_done", "intra_done",
                 "ox_ready", "comb_done", "rd_step", "rd_ready", "yn_done", "wo_done", "x_added", "su_done", "ks_done",
                 "sd_done", "supd_done")
        (ktz_zero, xc_ready, proj_done, elu_done, v_done, exp_done, yt_done, yt_copied, kt_done,
         kt_copied, lb_done, at_done, expd_done, neg_done, w_done, inter_done, intra_done,
         ox_ready, comb_done, rd_step, rd_ready, yn_done, wo_done, x_added, su_done, ks_done,
         sd_done, supd_done) = map(sem, names)

        with nc.Block() as block:
            @block.tensor
            def _(pe):
                def project_natural(b, bank, W, c):
                    nc.tensor.matmul(PA[:, bank, :], xc[:, b], W[:, c * 512:(c + 1) * 512], start=True, stop=True)\
                      .then_inc(proj_done, 1)

                def keys(n, b):
                    pe.wait_ge(xc_ready, n + 1)
                    for c in range(2):
                        if from_(n, 1):
                            pe.wait_ge(elu_done, n * 4 + (c - 1))
                        project_natural(b, c, WK, c)

                def values(n, b, c):
                    pe.wait_ge(elu_done, n * 4 + (c + 1))
                    project_natural(b, c, WV, c)

                def queries(n, b, c):
                    pe.wait_ge(v_done, n * 2 + (c + 1))
                    for j in range(4):
                        hp = 4 * c + j
                        last = nc.tensor.matmul(PA[:, c, j * P:(j + 1) * P], WQ[:, hp * P:(hp + 1) * P], xc[:, b],
                                                start=True, stop=True)
                    last.then_inc(proj_done, 1)

                def keys_turn(n, b, c):
                    if c:
                        pe.wait_ge(kt_copied, n * 2 + 1)
                    else:
                        pe.wait_ge(elu_done, n * 4 + 2)
                        if from_(n, 2):
                            pe.wait_ge(yt_copied, (n - 1) * 2)
                        elif n == 1:
                            pe.wait_ge(kt_copied, 2)
                    for j in range(4):
                        hp = 4 * c + j
                        last = nc.tensor.transpose(TR[:, j], Kn[:, b, hp * P:(hp + 1) * P], ident[:])
                    last.then_inc(kt_done, 1)

                def outputs_turn(t, c):
                    if c:
                        pe.wait_ge(yt_copied, t * 2 + 1)
                    else:
                        pe.wait_ge(yn_done, t + 1)
                        pe.wait_ge(kt_copied, t * 2 + 4 if not isinstance(t, int) or t < NT - 1 else 2 * NT)
                    for j in range(4):
                        hp = 4 * c + j
                        last = nc.tensor.transpose(TR[:, j], YN[:, hp * P:(hp + 1) * P], ident[:])
                    last.then_inc(yt_done, 1)

                def project_out(t, half_updates):
                    pe.wait_ge(yt_copied, t * 2 + 2)
                    pe.wait_ge(supd_done, half_updates)
                    for hp in range(HP):
                        last = nc.tensor.matmul(SU[:, 0:D], YTS[:, hp], WO[:, hp], start=(hp == 0), stop=(hp == HP - 1))
                    last.then_inc(wo_done, 1)

                def decays(t, b, i):
                    if i or from_(t, 1):
                        pe.wait_ge(expd_done, t * 4 + i)
                    nc.tensor.matmul(LB[:], identb[:], later[:].unsqueeze(1).to_broadcast([P, 4, P]),
                                     start=True, stop=False)
                    for j in range(4):
                        last = nc.tensor.matmul(LB[:, j], pick[:, 4 * i + j],
                                                LT[:, bass.ds(t, 1), :].rearrange("p o n -> p (o n)"),
                                                start=False, stop=(j == 3))
                    last.then_inc(lb_done, 1)

                def scores(t, b, i):
                    if i or from_(t, 1):
                        pe.wait_ge(w_done, t * 4 + i)
                    if i % 2 == 0:
                        pe.wait_ge(kt_copied, t * 2 + (1 + i // 2))
                        pe.wait_ge(elu_done, t * 4 + (3 + i // 2))
                    for j in range(4):
                        h = 4 * i + j
                        last = nc.tensor.matmul(AT[:, j], KTZ[:, b, h // 2, h % 2, :], QT[:, b, h // 2, :],
                                                start=True, stop=True)
                    last.then_inc(at_done, 1)

                def across_chunks(t, b, i):
                    if i or from_(t, 1):
                        pe.wait_ge(comb_done, t * 4 + i)
                    if from_(t, 1) and i % 2 == 0:
                        pe.wait_ge(supd_done, t * 2 + (i // 2 - 1))
                    for j in range(2):
                        hp = 2 * i + j
                        last = nc.tensor.matmul(OX[:, 2 * j * VW:2 * (j + 1) * VW], QT[:, b, hp, :],
                                                S[:, hp].rearrange("p h v -> p (h v)"), start=True, stop=True)
                    last.then_inc(inter_done, 1)

                def within_chunk(t, b, i):
                    pe.wait_ge(w_done, t * 4 + (i + 1))
                    for j in range(4):
                        h = 4 * i + j
                        last = nc.tensor.matmul(OI[:, j * VW:(j + 1) * VW], WB[:, i % 2, j, :], V1[:, b, h, :],
                                                start=True, stop=True)
                    last.then_inc(intra_done, 1)

                def state(t, b, c):
                    if c == 0:
                        pe.wait_ge(ks_done, t + 1)
                        if from_(t, 1):
                            pe.wait_ge(supd_done, t * 2)
                    elif from_(t, 1):
                        pe.wait_ge(x_added, t)
                    else:
                        pe.wait_ge(supd_done, 1)
                    for j in range(4):
                        for h in range(2):
                            hh = 2 * (4 * c + j) + h
                            last = nc.tensor.matmul(SU[64 * h:64 * h + 64, j * VW:(j + 1) * VW],
                                                    KS[:, b, hh * DH:(hh + 1) * DH], V1[:, b, hh, :],
                                                    start=True, stop=True)
                    last.then_inc(su_done, 1)

                def slot(t, b, i, last=False):
                    if i < 3:
                        decays(t, b, i + 1)
                    elif not last:
                        decays(t + 1, 1 - b, 0)
                    across_chunks(t, b, i)
                    within_chunk(t, b, i)
                    if i < 3:
                        scores(t, b, i + 1)
                    elif not last:
                        scores(t + 1, 1 - b, 0)

                def step(t, b, last=False):
                    first = isinstance(t, int) and t == 0
                    n, nb = t + 1, 1 - b
                    slot(t, b, 0)
                    if not first:
                        state(t - 1, nb, 1)
                    if not last:
                        keys(n, nb)
                    slot(t, b, 1)
                    state(t, b, 0)
                    for c in range(2):
                        if not last:
                            values(n, nb, c)
                        if not first:
                            outputs_turn(t - 1, c)
                    slot(t, b, 2)
                    for c in range(2):
                        if not last:
                            keys_turn(n, nb, c)
                            queries(n, nb, c)
                    slot(t, b, 3, last)
                    if not first:
                        project_out(t - 1, t * 2 + 1)

                pe.wait_ge(ktz_zero, 1)
                keys(0, 0)
                for c in range(2):
                    values(0, 0, c)
                for c in range(2):
                    keys_turn(0, 0, c)
                    queries(0, 0, c)
                decays(0, 0, 0)
                scores(0, 0, 0)
                step(0, 0)
                step(1, 1)
                over_pairs(pe, 2, NT - 1, step)
                step(NT - 1, (NT - 1) % 2, last=True)
                for c in range(2):
                    outputs_turn(NT - 1, c)
                pe.wait_ge(x_added, NT - 1)
                project_out(NT - 1, 2 * NT - 1)

            @block.scalar
            def _(act):
                def exp_(n, k, j):
                    act.wait_ge(proj_done, n * 6 + (j + 1))
                    if from_(n, 1):
                        act.wait_ge(elu_done, n * 4 + (k - 3))
                    nc.scalar.activation(enegs[:, k], PA[:, j % 2], ACT.Relu, scale=-1.0).then_inc(neg_done, 1)
                    act.wait_ge(neg_done, n * 4 + (k + 1))
                    nc.scalar.activation(etmp[:, k], enegs[:, k], ACT.Exp, scale=-1.0).then_inc(exp_done, 1)

                def v_copy(n, b, c):
                    act.wait_ge(proj_done, n * 6 + (3 + c))
                    if from_(n, 2):
                        act.wait_ge(intra_done, (n - 1) * 4)
                        act.wait_ge(su_done, (n - 1) * 2)
                    nc.scalar.activation(V1[:, b, 8 * c:8 * c + 8, 0:DH], PA[:, c].rearrange("p (h v) -> p h v", v=DH),
                                         ACT.Copy).then_inc(v_done, 1)

                def kt_copy(n, b, c):
                    act.wait_ge(kt_done, n * 2 + (c + 1))
                    if from_(n, 2):
                        act.wait_ge(at_done, (n - 1) * 4)
                    for h in range(2):
                        q = slice(64 * h, 64 * h + 64)
                        last = nc.scalar.activation(KTZ[q, b, 4 * c:4 * c + 4, h, :], TR[q], ACT.Copy)
                    last.then_inc(kt_copied, 1)

                def yt_copy(t, c):
                    act.wait_ge(yt_done, t * 2 + (c + 1))
                    if from_(t, 1):
                        act.wait_ge(wo_done, t)
                    nc.scalar.activation(YTS[:, 4 * c:4 * c + 4], TR[:], ACT.Copy).then_inc(yt_copied, 1)

                def exp_decay(t, b, i):
                    act.wait_ge(lb_done, t * 4 + (i + 1))
                    if i == 0:
                        act.wait_ge(xc_ready, t + 1)
                    if i >= 2 or from_(t, 1):
                        act.wait_ge(w_done, t * 4 + (i - 1))
                    for j in range(4):
                        h = 4 * i + j
                        last = nc.scalar.activation(DM[:, i % 2, j], LB[:, j], ACT.Exp, bias=nlc[:, b, h:h + 1])
                    last.then_inc(expd_done, 1)

                def step(t, b, last=False):
                    first = isinstance(t, int) and t == 0
                    n, nb = t + 1, 1 - b
                    exp_decay(t, b, 1)
                    if not last:
                        exp_(n, 0, 0)
                        exp_(n, 1, 1)
                    exp_decay(t, b, 2)
                    for c in range(2):
                        if not last:
                            v_copy(n, nb, c)
                        if not first:
                            yt_copy(t - 1, c)
                    exp_decay(t, b, 3)
                    if not last:
                        for c in range(2):
                            kt_copy(n, nb, c)
                            exp_(n, 2 + c, 4 + c)
                        exp_decay(n, nb, 0)

                act.wait_ge(ktz_zero, 1)
                exp_(0, 0, 0)
                exp_(0, 1, 1)
                v_copy(0, 0, 0)
                v_copy(0, 0, 1)
                for c in range(2):
                    kt_copy(0, 0, c)
                    exp_(0, 2 + c, 4 + c)
                exp_decay(0, 0, 0)
                step(0, 0)
                step(1, 1)
                over_pairs(act, 2, NT - 1, step)
                step(NT - 1, (NT - 1) % 2, last=True)
                yt_copy(NT - 1, 0)
                yt_copy(NT - 1, 1)

            @block.gpsimd
            def _(pool):
                def x_copy(n, b):
                    if from_(n, 2):
                        pool.wait_ge(proj_done, (n - 1) * 6)
                        pool.wait_ge(expd_done, (n - 1) * 4)
                    nc.gpsimd.tensor_copy(xc[:, b], XNT[:, bass.ds(n * P, P)])
                    nc.gpsimd.tensor_copy(nlc[:, b], nL[:, bass.ds(n, 1), :].rearrange("p o h -> p (o h)"))\
                      .then_inc(xc_ready, 1)

                def keys_decayed(t, b):
                    pool.wait_ge(elu_done, t * 4 + 2)
                    if from_(t, 2):
                        pool.wait_ge(su_done, (t - 1) * 2)
                    nc.gpsimd.tensor_tensor(KS[:, b].rearrange("p (h v) -> p h v", v=DH),
                                            Kn[:, b].rearrange("p (h v) -> p h v", v=DH),
                                            wk[:, bass.ds(t, 1), :].rearrange("p o h -> p (o h)").unsqueeze(2)
                                            .to_broadcast([P, H, DH]), ALU.mult).then_inc(ks_done, 1)

                def state_decayed(t, c):
                    if from_(t, 1):
                        pool.wait_ge(supd_done, t * 2 + (c - 1))
                    q = slice(4 * c, 4 * c + 4)
                    nc.gpsimd.tensor_tensor(SD[:, q].rearrange("p k h v -> p k (h v)"),
                                            S[:, q].rearrange("p k h v -> p k (h v)"),
                                            dec[:, bass.ds(t, 1), q].rearrange("p o h -> p (o h)").unsqueeze(2)
                                            .to_broadcast([P, 4, 2 * VW]), ALU.mult).then_inc(sd_done, 1)

                def divide(t, b):
                    pool.wait_ge(rd_ready, t + 1)
                    if from_(t, 1):
                        pool.wait_ge(yt_done, t * 2)
                    nc.gpsimd.tensor_tensor(YN[:].rearrange("p (h v) -> p h v", v=DH), O[:, b, :, 0:DH],
                                            rd[:].unsqueeze(2).to_broadcast([P, H, DH]), ALU.mult).then_inc(yn_done, 1)

                def step(t, b, last=False, copy=True):
                    first = isinstance(t, int) and t == 0
                    if not first:
                        divide(t - 1, 1 - b)
                    state_decayed(t, 1)
                    if not last:
                        keys_decayed(t + 1, 1 - b)
                        state_decayed(t + 1, 0)
                    if copy:
                        x_copy(t + 2, b)

                nc.gpsimd.memset(KTZ[:], 0.0).then_inc(ktz_zero, 1)
                x_copy(0, 0)
                x_copy(1, 1)
                state_decayed(0, 0)
                keys_decayed(0, 0)
                step(0, 0)
                step(1, 1)
                over_pairs(pool, 2, NT - 2, step)
                step(NT - 2, (NT - 2) % 2, copy=False)
                step(NT - 1, (NT - 1) % 2, last=True, copy=False)
                divide(NT - 1, (NT - 1) % 2)

            @block.vector
            def _(dve):
                def elu(n, k, j, dst):
                    dve.wait_ge(exp_done, n * 4 + (k + 1))
                    nc.vector.scalar_tensor_tensor(out=dst, in0=PA[:, j % 2], scalar=0.0, in1=etmp[:, k], op0=ALU.max,
                                                   op1=ALU.add).then_inc(elu_done, 1)

                def elu_keys(n, b):
                    if from_(n, 2):
                        dve.wait_ge(kt_done, (n - 1) * 2)
                        dve.wait_ge(ks_done, n - 1)
                    for c in range(2):
                        elu(n, c, c, Kn[:, b, c * 512:(c + 1) * 512])

                def elu_queries(n, b):
                    if from_(n, 2):
                        dve.wait_ge(inter_done, (n - 1) * 4)
                    for c in range(2):
                        elu(n, 2 + c, 4 + c, QT[:, b, 4 * c:4 * c + 4].rearrange("p k q -> p (k q)"))

                def weigh(t, i):
                    dve.wait_ge(expd_done, t * 4 + (i + 1))
                    dve.wait_ge(at_done, t * 4 + (i + 1))
                    if i >= 2 or from_(t, 1):
                        dve.wait_ge(intra_done, t * 4 + (i - 1))
                    nc.vector.tensor_tensor(WB[:, i % 2], AT[:], DM[:, i % 2], ALU.mult).then_inc(w_done, 1)

                def combine(t, b, i):
                    dve.wait_ge(intra_done, t * 4 + (i + 1))
                    if i == 0 and from_(t, 2):
                        dve.wait_ge(yn_done, t - 1)
                    nc.vector.tensor_tensor(ox[:], OX[:, 0:4 * VW].rearrange("p (h v) -> p h v", v=VW),
                                            eL[:, bass.ds(t, 1), 4 * i:4 * i + 4].rearrange("p o h -> p (o h)")
                                            .unsqueeze(2).to_broadcast([P, 4, VW]), ALU.mult).then_inc(ox_ready, 1)
                    dve.wait_ge(ox_ready, t * 4 + (i + 1))
                    nc.vector.tensor_tensor(O[:, b, 4 * i:4 * i + 4].rearrange("p h v -> p (h v)"), OI[:, 0:4 * VW],
                                            ox[:].rearrange("p h v -> p (h v)"), ALU.add).then_inc(comb_done, 1)

                def reciprocals(t, b):
                    dve.wait_ge(comb_done, t * 4 + 4)
                    if from_(t, 1):
                        dve.wait_ge(yn_done, t)
                    nc.vector.tensor_scalar_add(rd[:], O[:, b, :, DH], EPS).then_inc(rd_step, 1)
                    dve.wait_ge(rd_step, t + 1)
                    nc.vector.reciprocal(rd[:], rd[:]).then_inc(rd_ready, 1)

                def update(t, c):
                    dve.wait_ge(su_done, t * 2 + (c + 1))
                    dve.wait_ge(sd_done, t * 2 + (c + 1))
                    dve.wait_ge(inter_done, t * 4 + (2 * c + 2))
                    for h in range(2):
                        q = slice(64 * h, 64 * h + 64)
                        last = nc.vector.tensor_tensor(S[q, 4 * c:4 * c + 4, h, :],
                                                       SU[q, 0:4 * VW].rearrange("p (k v) -> p k v", v=VW),
                                                       SD[q, 4 * c:4 * c + 4, h, :], ALU.add)
                    last.then_inc(supd_done, 1)

                def add_out(t):
                    dve.wait_ge(wo_done, t + 1)
                    xs = X[:, bass.ds(t, 1), :].rearrange("p o d -> p (o d)")
                    nc.vector.tensor_tensor(xs, xs, SU[:, 0:D], ALU.add).then_inc(x_added, 1)

                def step(t, b, last=False):
                    first = isinstance(t, int) and t == 0
                    n, nb = t + 1, 1 - b
                    combine(t, b, 0)
                    weigh(t, 1)
                    if not first:
                        update(t - 1, 1)
                    if not last:
                        elu_keys(n, nb)
                    combine(t, b, 1)
                    weigh(t, 2)
                    update(t, 0)
                    combine(t, b, 2)
                    weigh(t, 3)
                    if not last:
                        elu_queries(n, nb)
                    combine(t, b, 3)
                    reciprocals(t, b)
                    if not last:
                        weigh(n, 0)
                    if not first:
                        add_out(t - 1)

                elu_keys(0, 0)
                elu_queries(0, 0)
                weigh(0, 0)
                step(0, 0)
                step(1, 1)
                over_pairs(dve, 2, NT - 1, step)
                step(NT - 1, (NT - 1) % 2, last=True)
                add_out(NT - 1)


def program(nc, io, out, upto="all"):
    NT = 16
    with ExitStack() as ctx:
        X = ctx.enter_context(nc.sbuf_tensor("X", [P, NT, P], F32))
        W3 = ctx.enter_context(nc.sbuf_tensor("W3", [P, 3 * Router.E * Router.FF], F32))
        experts_loaded = ctx.enter_context(nc.semaphore("experts_loaded"))
        ident = ctx.enter_context(nc.sbuf_tensor("ident", [P, P], F32))
        identb = ctx.enter_context(nc.sbuf_tensor("identb", [P, P], BF16))
        ident_zero = ctx.enter_context(nc.semaphore("ident_zero"))
        out_stored = ctx.enter_context(nc.semaphore("out_stored"))
        scratch = {"qk": nc.dram_tensor("qk_parts", [2, 3, 8, 16, 2, 2, 1024], BF16, kind="Internal"),
                   "xn": nc.dram_tensor("xn_rows", [NT * P, P], F32, kind="Internal"),
                   "yd": nc.dram_tensor("yd_rows", [2 * NT * P + Router.SLOTS * P, P], F32, kind="Internal")}
        with nc.Block() as block:
            @block.gpsimd
            def _(pool):
                nc.gpsimd.memset(ident[:], 0.0).then_inc(ident_zero, 1)
                nc.gpsimd.memset(identb[:], 0.0).then_inc(ident_zero, 1)
                pool.wait_ge(ident_zero, 2)
                for m in (ident, identb):
                    nc.gpsimd.affine_select(out=m[:], in_=m[:], compare_op=ALU.not_equal, fill=1.0, base=0,
                                            pattern=[[-1, P]], channel_multiplier=1).then_inc(ident_zero, 1)
        a = {n[len("L0_attn_a_"):]: ap for n, ap in io.items() if n.startswith("L0_attn_a_")}
        f = {n[len("L0_ffn_"):]: ap for n, ap in io.items() if n.startswith("L0_ffn_")}
        with nc.cleanup_on_exit():
            diff_attention(nc, X, W3, ident, identb, a, scratch,
                           lambda sp: load_experts(nc, sp, W3, f, experts_loaded))
        if upto != "attn_a":
            with nc.cleanup_on_exit():
                moe(nc, "m1", X, W3, ident, f, scratch, experts_loaded)
        if upto not in ("attn_a", "ffn1"):
            d = {n[len("L0_attn_b_"):]: ap for n, ap in io.items() if n.startswith("L0_attn_b_")}
            with nc.cleanup_on_exit():
                decay_attention(nc, X, ident, identb, d)
        if upto == "all":
            with nc.cleanup_on_exit():
                moe(nc, "m2", X, W3, ident, f, scratch, experts_loaded)
        with nc.Block() as block:
            @block.sync
            def _(sp):
                sp.dma_start(out.rearrange("b (t p) d -> p (b t) d", p=P), X[:]).then_inc(out_stored, 16)
                sp.wait_ge(out_stored, 16)


_INS = ["L0_attn_a_x", "L0_attn_a_Wq1", "L0_attn_a_Wq2", "L0_attn_a_Wk1", "L0_attn_a_Wk2", "L0_attn_a_Wv", "L0_attn_a_Wc",
        "L0_attn_a_lq1", "L0_attn_a_lk1", "L0_attn_a_lq2", "L0_attn_a_lk2", "L0_attn_b_Wq", "L0_attn_b_Wk", "L0_attn_b_Wv",
        "L0_attn_b_Wo", "L0_attn_b_Wa", "L0_attn_b_ba", "L0_ffn_router_w", "L0_ffn_w_gate", "L0_ffn_w_up",
        "L0_ffn_w_down"]


def kernel(**inputs):
    import numpy as _np
    import concourse.bacc as _bacc
    from concourse.bass_utils import run_bass_kernel_spmd as _run

    nc = _bacc.Bacc("TRN2", target_bir_lowering=False, num_devices=1)
    arrays, io = {}, {}
    for name in _INS:
        a = _np.ascontiguousarray(inputs[name])
        arrays[f"in_{name}"] = a
        io[name] = nc.dram_tensor(f"in_{name}", a.shape, mybir.dt.from_np(a.dtype), kind="ExternalInput").ap()
    out = nc.dram_tensor("out_x", (2, 1024, 128), F32, kind="ExternalOutput").ap()
    program(nc, io, out)
    r = _run(nc, [arrays], core_ids=[0])
    return r.results[0]["out_x"]
```
